# Optimizing a Trainium2 kernel written in Bass

```python
import numpy as np
import jax
import jax.numpy as jnp

def _softmax(x, axis=-1):
    return jax.nn.softmax(x, axis=axis)

def _gelu(x):
    return jax.nn.gelu(x, approximate=True)

def _silu(x):
    return jax.nn.silu(x)

def _sigmoid(x):
    return jax.nn.sigmoid(x)

def _layernorm(x, axis=-1, eps=1e-05):
    m = jnp.mean(x, axis=axis, keepdims=True)
    v = jnp.var(x, axis=axis, keepdims=True)
    return (x - m) / jnp.sqrt(v + eps)

def _scatter_add(tgt, idx, src, axis=0):
    return tgt.at[idx].add(src)

def _segment_sum(src, seg, n):
    return jax.ops.segment_sum(src, seg, n)
kernel_name = 'mk_xattn_ffn_d1_seqx_r8_c8319c'

def setup_inputs(seed: int=0):
    np.random.seed(seed)
    _w = jnp.asarray

    def _rec_inputs():
        import jax
        import jax.numpy as jnp
        _rk = jax.random.key(seed)
        x = -0.0003929 + 0.9999 * jax.random.normal(jax.random.fold_in(_rk, 1), (16, 64, 512), jnp.float32)
        _lenS = 64 - jax.random.randint(jax.random.fold_in(_rk, 7), (16,), 0, max(1, 64 // 4) + 1, jnp.int32)
        _lenS2 = 64 - jax.random.randint(jax.random.fold_in(_rk, 8), (16,), 0, max(1, 64 // 4) + 1, jnp.int32)
        _ctx_1024P = jax.random.normal(jax.random.fold_in(_rk, 11), (16, 16, 128), jnp.float32)
        _ctx_1024c = jax.random.dirichlet(jax.random.fold_in(_rk, 511), 0.3 * jnp.ones((16,), jnp.float32), (16, 64))
        _ctx_1024t = jnp.einsum('bsk,bkd->bsd', _ctx_1024c, _ctx_1024P)
        _ctx_1024t = _ctx_1024t * jax.lax.rsqrt(jnp.mean(jnp.square(_ctx_1024t)) + 1e-12) * 0.953939
        ctx_1024 = -1.39393e-06 + 0.999914 * (_ctx_1024t + 0.3 * jax.random.normal(jax.random.fold_in(_rk, 611), (16, 64, 128), jnp.float32))
        return (x, ctx_1024)
    x, ctx_1024 = _rec_inputs()

    def _L0_xattn_setup():
        import jax, jax.numpy as jnp
        import numpy as np
        import math
        DIM_V = 64
        key = jax.random.key(seed)
        k1, k2, k3, k4, k5, k6 = jax.random.split(key, 6)
        B, C, N, M = (8, DIM_V, 512, 128)
        pcd_up = jax.random.normal(k1, (B, C, N), dtype=jnp.float32)
        pcd_down = jax.random.normal(k2, (B, C, M), dtype=jnp.float32)
        s = 1.0 / math.sqrt(C)
        Wq = jax.random.normal(k3, (C, C), dtype=jnp.float32) * s
        Wk = jax.random.normal(k4, (C, C), dtype=jnp.float32) * s
        Wv = jax.random.normal(k5, (C, C), dtype=jnp.float32) * s
        Wskip = jax.random.normal(k6, (C, C), dtype=jnp.float32) * s
        return {'pcd_up': pcd_up, 'pcd_down': pcd_down, 'Wq': Wq, 'Wk': Wk, 'Wv': Wv, 'Wskip': Wskip}
    _L0_xattn_all = _L0_xattn_setup()
    _L0_xattn_in = {k: v for k, v in _L0_xattn_all.items() if k in ('Wq', 'Wk', 'Wv', 'Wskip')}
    del _L0_xattn_all

    def _L0_ffn_setup():
        import jax, jax.numpy as jnp
        import numpy as np
        TOP_K = 2
        key = jax.random.key(seed)
        k0, k1, k2 = jax.random.split(key, 3)
        B, S, D, H, E = (4, 256, 512, 512, 8)
        sc = 1.0 / np.sqrt(D).astype(np.float32)
        x = jax.random.normal(k0, (B, S, D), dtype=jnp.float32)
        W_gate = jax.random.normal(k1, (D, E), dtype=jnp.float32) * sc
        b_gate = jnp.zeros((E,), dtype=jnp.float32)
        W_e = jax.random.normal(k2, (E, D, H), dtype=jnp.float32) * sc
        b_e = jnp.zeros((E, H), dtype=jnp.float32)
        return {'x': x, 'W_gate': W_gate, 'b_gate': b_gate, 'W_e': W_e, 'b_e': b_e}
    _L0_ffn_all = _L0_ffn_setup()
    _L0_ffn_in = {k: v for k, v in _L0_ffn_all.items() if k in ('W_gate', 'b_gate', 'W_e', 'b_e')}
    del _L0_ffn_all
    return {'x': x, 'ctx_1024': ctx_1024, 'L0_xattn_Wq': _L0_xattn_in['Wq'], 'L0_xattn_Wk': _L0_xattn_in['Wk'], 'L0_xattn_Wv': _L0_xattn_in['Wv'], 'L0_xattn_Wskip': _L0_xattn_in['Wskip'], 'L0_ffn_W_gate': _L0_ffn_in['W_gate'], 'L0_ffn_b_gate': _L0_ffn_in['b_gate'], 'L0_ffn_W_e': _L0_ffn_in['W_e'], 'L0_ffn_b_e': _L0_ffn_in['b_e']}

def reference(x, ctx_1024, L0_xattn_Wq, L0_xattn_Wk, L0_xattn_Wv, L0_xattn_Wskip, L0_ffn_W_gate, L0_ffn_b_gate, L0_ffn_W_e, L0_ffn_b_e):
    import jax
    import jax.numpy as jnp

    def _L0_xattn_ref(pcd_up, pcd_down, Wq, Wk, Wv, Wskip):
        import jax, jax.numpy as jnp
        import numpy as np
        import math
        DIM_V = 64
        q = jnp.einsum('oc,bcn->bon', Wq, pcd_up)
        k = jnp.einsum('oc,bcm->bom', Wk, pcd_down)
        v = jnp.einsum('oc,bcm->bom', Wv, pcd_down)
        C = q.shape[1]
        scale = jnp.sqrt(jnp.asarray(C, dtype=q.dtype))
        energy = jnp.einsum('bcn,bcm->bnm', q, k) / scale
        attention = jax.nn.softmax(energy, axis=-1)
        x = jnp.einsum('bnm,bcm->bcn', attention, v)
        skip = jnp.einsum('oc,bcn->bon', Wskip, pcd_up)
        return skip + x

    def _L0_ffn_ref(x, W_gate, b_gate, W_e, b_e):
        import jax, jax.numpy as jnp
        import numpy as np
        TOP_K = 2
        logits = x @ W_gate + b_gate
        _, top_idx = jax.lax.top_k(logits, TOP_K)
        y_all = jax.nn.relu(jnp.einsum('bsd,edh->bseh', x, W_e) + b_e)
        y = jnp.take_along_axis(y_all, top_idx[..., None], axis=2)
        return y.mean(axis=2)
    x = x + _L0_xattn_ref(_layernorm(x, axis=-1), ctx_1024, L0_xattn_Wq, L0_xattn_Wk, L0_xattn_Wv, L0_xattn_Wskip)
    x = x + _L0_ffn_ref(_layernorm(x, axis=-1), L0_ffn_W_gate, L0_ffn_b_gate, L0_ffn_W_e, L0_ffn_b_e)
    return x

_drawn_inputs = setup_inputs


def setup_inputs(seed=0):
    import zlib

    import numpy as np

    out = dict(_drawn_inputs(seed))
    spreads = {'L0_ffn_b_gate': (0.0, 0.1), 'L0_ffn_b_e': (0.0, 0.1)}
    factors = {}
    for name, (base, spread) in spreads.items():
        noise = np.random.default_rng([zlib.crc32(name.encode()), seed]).standard_normal(out[name].shape)
        drawn = base * np.exp(spread * noise) if base else spread * noise
        out[name] = jnp.asarray(drawn.astype(out[name].dtype))
    for name, factor in factors.items():
        out[name] = (out[name] * factor).astype(out[name].dtype)
    return out
```

```python
from contextlib import ExitStack

import concourse.bass as bass
from concourse import mybir

P = 128
ALU = mybir.AluOpType
ACT = mybir.ActivationFunctionType
F32 = mybir.dt.float32
F16 = mybir.dt.float16
I32 = mybir.dt.int32
BF16 = mybir.dt.bfloat16
F32R = mybir.dt.float32r
AX = mybir.AxisListType
EPS = 1e-5


def build_xattn_moe(nc, x, ctx_in, Wq, Wk, Wv, Wskip, W_gate, b_gate, W_e, b_e, out):
    B, C, D = x.shape
    M = ctx_in.shape[2]
    E, _, H = W_e.shape
    PAIR = P // C
    NT = B // PAIR
    NCH = D // P
    NQ = PAIR * NCH
    TOKENS = B * C
    TOPK = 2
    SLOT_TILES = TOKENS * TOPK // P + E - 1
    ST = SLOT_TILES + 1
    assert M == P and PAIR == 2 and D == H == 512 and NT == E == 8
    SKIPPED = 1 << 20

    x_t = x.rearrange("(t j) c d -> t (j c) d", j=PAIR)
    out_t = out.rearrange("(t j) c d -> t (j c) d", j=PAIR)
    ctx_t = ctx_in.rearrange("(t j) c m -> j c t m", j=PAIR)
    rows2 = nc.dram_tensor("normed_rows", (TOKENS, D), F32, kind="Internal").ap()
    rows_y = nc.dram_tensor("expert_rows", (TOPK * TOKENS, H), F32, kind="Internal").ap()

    bias_rows = nc.dram_tensor("bias_rows", (3, E, H), BF16, kind="Internal").ap()
    PIECES = 4

    with ExitStack() as stack:
        def sb(name, shape, dt=F32):
            return stack.enter_context(nc.sbuf_tensor(name, shape, dt))

        def sem(name):
            return stack.enter_context(nc.semaphore(name))

        def over_at(name, host, start, shape, dt=F32):
            return nc.alloc_sbuf_tensor_at(name, shape, dt, offset=host_at[host] + start)

        host_at = {}

        def host(name, shape, dt=F32):
            host_at[name] = nc.sbuf_base
            return sb(name, shape, dt)

        res = sb("res", [P, NT, D])
        w_hi = sb("w_hi", [P, E, NCH, H], F32R)
        w_lo = sb("w_lo", [P, E, NCH, H], F32R)
        w_raw = host("w_raw", [P, 2, NCH, H])
        ctx_diag = host("ctx_diag", [P, NT, PAIR, M])
        w_small = sb("w_small", [C, 4, 2, C])
        at_diag = sb("at_diag", [P, P])
        wv_diag = sb("wv_diag", [P, P])
        wskip_diag = sb("wskip_diag", [P, P])
        xn = host("xn", [P, 2, D])
        kk = sb("kk", [P, 2, PAIR * M])
        vext = sb("vext", [P, 3, PAIR, P])
        probs = host("probs", [P, 2, NCH, PAIR, M])
        be_left = [over_at(f"be_left{i}", "probs", i * H * 4, [E, H]) for i in range(2)]
        be_part = over_at("be_part", "probs", 2 * H * 4, [E, 3, H], BF16)
        probsT = host("probsT", [P, PAIR, D])
        stats = sb("stats", [P, 2, 6])
        mv = sb("mv", [P, 2, 2])
        rstd = sb("rstd", [P, 2, 1])
        stats2 = sb("stats2", [P, 2, 6])
        mv2 = sb("mv2", [P, 2, 2])
        rstd2 = sb("rstd2", [P, 2, 1])
        negmax = sb("negmax", [P, 2, NQ])
        rowsum = sb("rowsum", [P, 2, NQ])
        rinv = sb("rinv", [P, 2, NQ])
        xn2 = host("xn2", [P, 2, D])
        xn2T = sb("xn2T", [P, NCH, P])
        w_gate = sb("w_gate", [P, NCH, E])
        bg_rep = sb("bg_rep", [P, E])
        bias3 = over_at("bias3", "ctx_diag", 0, [3, E, H], BF16)
        logits = sb("logits", [P, E])
        top8 = sb("top8", [P, 8])
        top_idx = sb("top_idx", [P, 8], mybir.dt.uint32)
        top_f = sb("top_f", [P, 2])
        chosen = sb("chosen", [P, TOPK, E, NT], F16)
        both = sb("both", [P, E, NT], F16)
        ident = sb("ident", [P, P])
        ones3 = sb("ones3", [3, P], BF16)
        power = sb("power", [P, 1])
        ones_h = sb("ones_h", [P, P], F16)
        below_h = sb("below_h", [P, P], F16)
        iota_h = sb("iota_h", [P, P], F16)
        iota_e = sb("iota_e", [P, E])
        scan_keep = sb("scan_keep", [P, E * NT])
        steps128 = sb("steps128", [P, NT])
        iota_st = sb("iota_st", [P, ST])
        pair_no = sb("pair_no", [P, TOPK, NT])
        tile_cnt = sb("tile_cnt", [P, E, NT])
        incl = sb("incl", [P, E, NT])
        over = sb("over", [P, E, NT])
        ntile = sb("ntile", [P, E])
        tile_end = sb("tile_end", [P, E])
        slot0 = sb("slot0", [P, E, NT])
        slot_all = sb("slot_all", [P, E, NT])
        slot_sel = sb("slot_sel", [P, TOPK, NT, E])
        slot_f = sb("slot_f", [P, TOPK, NT])
        slot_i = sb("slot_i", [P, TOPK, NT], I32)
        hi_i = sb("hi_i", [P, TOPK, NT], I32)
        lo_i = sb("lo_i", [P, TOPK, NT], I32)
        hi_f = sb("hi_f", [P, TOPK, NT])
        lo_f = sb("lo_f", [P, TOPK, NT])
        lo_hot = over_at("lo_hot", "w_raw", 0, [P, TOPK, NT, P], F16)
        hi_eq = over_at("hi_eq", "w_raw", 4096, [P, TOPK * NT, ST])
        hi_hot = over_at("hi_hot", "w_raw", 4096 + 2048, [P, TOPK * NT, ST], F16)
        past = over_at("past", "w_raw", 4096 + 4096, [P, ST, E])
        exp_f = sb("exp_f", [P, ST])
        exp_i = sb("exp_i", [P, ST], I32)
        pair_f = sb("pair_f", [P, ST])
        empty_f = sb("empty_f", [P, ST])
        pair_i = sb("pair_i", [P, ST], I32)
        gather_i = sb("gather_i", [P, ST], I32)
        scat_f = sb("scat_f", [P, ST])
        scatter_i = sb("scatter_i", [P, ST], I32)
        NG = 4
        NY = 4
        xg = over_at("xg", "probs", 0, [P, NG, D])
        xgT_hi = over_at("xgT_hi", "xn", 0, [P, 2, D], F32R)
        xgT_lo = over_at("xgT_lo", "xn2", 0, [P, 2, D], F32R)
        ysb = over_at("ysb", "w_raw", 0, [P, NG, H])
        y_in = over_at("y_in", "w_raw", 0, [P, NY, TOPK, H])
        fin = over_at("fin", "probsT", 0, [P, 2, D])

        bank = [stack.enter_context(nc.psum_tensor(f"bank{i}", [P, 512], F32)) for i in range(4)]
        energy = stack.enter_context(nc.psum_tensor("energy", [P, 2, 512], F32))
        turned = stack.enter_context(nc.psum_tensor("turned", [P, PAIR, 512], F32))
        acc, gate_bank, kv_bank, small_bank = bank
        setup_bank = kv_bank

        x_in = [sem("x_in0"), sem("x_in1"), sem("x_in_rest")]
        ctx_in_s = sem("ctx_in_s")
        small_in = sem("small_in")
        gate_in = sem("gate_in")
        w_in = [sem(f"w_in{e}") for e in range(E)]
        consts = sem("consts")
        zeroed = sem("zeroed")
        set_ps = sem("set_ps")
        set_sb = sem("set_sb")
        mv_done = sem("mv_done")
        rstd_done = sem("rstd_done")
        xn_done = sem("xn_done")
        kv_ps = sem("kv_ps")
        kk_sb = sem("kk_sb")
        v_sb = sem("v_sb")
        energy_ps = sem("energy_ps")
        negmax_done = sem("negmax_done")
        exp_done = sem("exp_done")
        rinv_done = sem("rinv_done")
        probs_done = sem("probs_done")
        turned_ps = sem("turned_ps")
        turned_sb = sem("turned_sb")
        acc_ps = sem("acc_ps")
        acc_used = sem("acc_used")
        mv2_done = sem("mv2_done")
        rstd2_done = sem("rstd2_done")
        xn2_done = sem("xn2_done")
        rows2_out = [sem("rows2_out0"), sem("rows2_out1")]
        xn2T_ps = sem("xn2T_ps")
        xn2T_sb = sem("xn2T_sb")
        logits_ps = sem("logits_ps")
        logits_used = sem("logits_used")
        dve = sem("dve")
        both_done = sem("both_done")
        count_ps = sem("count_ps")
        pairs_ps = sem("pairs_ps")
        exp_ids = sem("exp_ids")
        slots_done = sem("slots_done")
        gathered = [sem(f"gathered{i}") for i in range(NG)]
        xgT_ps = sem("xgT_ps")
        y_ps = sem("y_ps")
        y_sb = sem("y_sb")
        scattered = [sem(f"scattered{i}") for i in range(NG)]
        y_back = [sem(f"y_back{i}") for i in range(NY)]
        be_in = sem("be_in")
        be_parts = sem("be_parts")
        be_dram = sem("be_dram")
        bias_in = sem("bias_in")
        hi_split = sem("hi_split")
        lo_split = sem("lo_split")
        slots_known = sem("slots_known")
        lo_hot_pool = sem("lo_hot_pool")
        lo_hot_dve = sem("lo_hot_dve")
        hi_hot_done = sem("hi_hot_done")
        hi_turned = sem("hi_turned")
        lo_turned = sem("lo_turned")
        fin_part = sem("fin_part")
        fin_done = sem("fin_done")
        out_done = [sem("out_done0"), sem("out_done1")]

        N_CONST = 12
        tick = [0]

        block = stack.enter_context(nc.Block())

        def x_ready(eng, t):
            eng.wait_ge(x_in[min(t, 2)], 16)

        @block.sync
        def _(sp):
            def store_rows(t):
                sp.wait_ge(xn2_done, t + 1)
                sp.dma_start(rows2[t * P:(t + 1) * P, :], xn2[:, t % 2, :]).then_inc(rows2_out[t % 2], 16)

            for i, w in enumerate((Wq, Wk, Wv, Wskip)):
                for r in range(2):
                    sp.dma_start(w_small[:, i, r, :], w).then_inc(small_in, 16)
            sp.dma_start(res[:, 0, :], x_t[0]).then_inc(x_in[0], 16)
            sp.wait_ge(zeroed, 1)
            for j in range(PAIR):
                sp.dma_start(ctx_diag[j * C:(j + 1) * C, :, j, :], ctx_t[j]).then_inc(ctx_in_s, 16)
            sp.dma_start(res[:, 1, :], x_t[1]).then_inc(x_in[1], 16)
            sp.dma_start(res[:, 2:NT, :], x_t[2:NT].rearrange("t p d -> p t d")).then_inc(x_in[2], 16)
            sp.dma_start(w_gate[:], W_gate.rearrange("(c p) e -> p c e", p=P)).then_inc(gate_in, 16)
            sp.dma_start(bg_rep[:], b_gate.rearrange("(a e) -> a e", a=1).to_broadcast([P, E])).then_inc(gate_in, 16)
            sp.dma_start(be_left[0][:], b_e).then_inc(be_in, 16)
            sp.wait_ge(be_parts, 3)
            sp.dma_start(bias_rows.rearrange("k e h -> e k h"), be_part[:]).then_inc(be_dram, 16)
            for e in range(E):
                if e >= 2:
                    sp.wait_ge(lo_split, PIECES * (e - 1))
                sp.dma_start(w_raw[:, e % 2, :, :], W_e[e].rearrange("(c p) h -> p c h", p=P)).then_inc(w_in[e], 16)
                if e >= 2:
                    store_rows(e - 2)
            for t in range(E - 2, NT):
                store_rows(t)
            sp.wait_ge(be_dram, 16)
            sp.wait_ge(kv_ps, NT)
            sp.dma_start(bias3[:], bias_rows).then_inc(bias_in, 16)
            for i in range(NG):
                sp.wait_ge(scattered[i], 16 * len(range(i, SLOT_TILES, NG)))
            for t in range(NT):
                if t >= NY:
                    sp.wait_ge(fin_done, t - NY + 1)
                for k in range(TOPK):
                    r = k * TOKENS + t * P
                    sp.dma_start(y_in[:, t % NY, k, :], rows_y[r:r + P, :]).then_inc(y_back[t % NY], 16)
            for i in range(2):
                sp.wait_ge(out_done[i], 16 * NT // 2)

        @block.gpsimd
        def _(pool):
            pool.memset(ctx_diag[:], 0.0).then_inc(zeroed, 1)
            pool.memset(power[:], -0.5).then_inc(consts, 1)
            pool.memset(ident[:], 0.0).then_inc(zeroed, 1)
            pool.memset(below_h[:], 1.0).then_inc(zeroed, 1)
            pool.memset(ones3[:], 1.0).then_inc(consts, 1)
            pool.memset(ones_h[:], 1.0).then_inc(consts, 1)
            pool.memset(scan_keep[:], 1.0).then_inc(zeroed, 1)
            pool.memset(at_diag[:], 0.0).then_inc(zeroed, 1)
            pool.memset(wv_diag[:], 0.0).then_inc(zeroed, 1)
            pool.memset(wskip_diag[:], 0.0).then_inc(zeroed, 1)
            pool.wait_ge(zeroed, 7)
            pool.affine_select(out=ident[:], in_=ident[:], compare_op=ALU.not_equal, fill=1.0, base=0,
                               pattern=[[-1, P]], channel_multiplier=1).then_inc(consts, 1)
            pool.affine_select(out=below_h[:], in_=below_h[:], compare_op=ALU.is_gt, fill=0.0, base=0,
                               pattern=[[1, P]], channel_multiplier=-1).then_inc(consts, 1)
            sk = scan_keep[:].rearrange("p (e t) -> p e t", t=NT)
            pool.affine_select(out=sk, in_=sk, compare_op=ALU.not_equal, fill=0.0, base=0,
                               pattern=[[0, E], [1, NT]], channel_multiplier=0).then_inc(consts, 1)
            pool.iota(iota_h[:], [[1, P]], base=0, channel_multiplier=0,
                      allow_small_or_imprecise_dtypes=True).then_inc(consts, 1)
            pool.iota(iota_e[:], [[1, E]], base=0, channel_multiplier=0,
                      allow_small_or_imprecise_dtypes=True).then_inc(consts, 1)
            pool.iota(steps128[:], [[P, NT]], base=0, channel_multiplier=0,
                      allow_small_or_imprecise_dtypes=True).then_inc(consts, 1)
            pool.iota(iota_st[:], [[1, ST]], base=0, channel_multiplier=0,
                      allow_small_or_imprecise_dtypes=True).then_inc(consts, 1)
            pool.iota(pair_no[:], [[TOKENS, TOPK], [P, NT]], base=1, channel_multiplier=1,
                      allow_small_or_imprecise_dtypes=True).then_inc(consts, 1)
            pool.iota(slot_f[:], [[1, TOPK * NT]], base=1, channel_multiplier=1,
                      allow_small_or_imprecise_dtypes=True).then_inc(consts, 1)
            pool.wait_ge(consts, 1)

            def root(mv_, rstd_, ready, done, t):
                pool.wait_ge(ready, t + 1)
                pool.tensor_tensor(rstd_[:, t % 2, :], mv_[:, t % 2, 1:2], power[:], ALU.pow).then_inc(done, 1)

            def split_lo(e):
                for c in range(PIECES):
                    pool.wait_ge(hi_split, PIECES * e + c + 1)
                    pool.tensor_tensor(w_lo[:, e, c, :], w_raw[:, e % 2, c, :], w_hi[:, e, c, :].bitcast(F32),
                                       ALU.subtract).then_inc(lo_split, 1)

            root(mv, rstd, mv_done, rstd_done, 0)
            root(mv, rstd, mv_done, rstd_done, 1)
            for t in range(NT):
                if t + 2 < NT:
                    root(mv, rstd, mv_done, rstd_done, t + 2)
                if t >= 1:
                    root(mv2, rstd2, mv2_done, rstd2_done, t - 1)
                split_lo(t)
            root(mv2, rstd2, mv2_done, rstd2_done, NT - 1)

            pool.wait_ge(slots_known, 1)
            for t in range(NT):
                pool.tensor_scalar(lo_hot[:, 1, t, :], iota_h[:], lo_f[:, 1, t:t + 1], None, ALU.is_equal).then_inc(lo_hot_pool, 1)
            pool.wait_ge(slots_done, 1)
            for i in range(2):
                pool.wait_ge(rows2_out[i], 16 * NT // 2)

            def gather(j):
                if j >= NG:
                    pool.wait_ge(xgT_ps, j - NG + 1)
                pool.indirect_dma_start(xg[:, j % NG, :], None, rows2,
                                        bass.IndirectOffsetOnAxis(gather_i[:, j:j + 1], 0)).then_inc(gathered[j % NG], 16)

            for j in range(NG):
                gather(j)
            for j in range(SLOT_TILES):
                pool.wait_ge(y_sb, j + 1)
                pool.indirect_dma_start(rows_y, bass.IndirectOffsetOnAxis(scatter_i[:, j:j + 1], 0),
                                        ysb[:, j % NG, :], None, bounds_check=TOPK * TOKENS - 1,
                                        oob_is_err=False).then_inc(scattered[j % NG], 16)
                if j + NG < SLOT_TILES:
                    gather(j + NG)

        @block.scalar
        def _(act):
            def kv_copy(t):
                act.wait_ge(kv_ps, t + 1)
                if t >= 2:
                    act.wait_ge(energy_ps, 2 * (t - 1))
                act.copy(kk[:, t % 2, :], kv_bank[:, 0:PAIR * M]).then_inc(kk_sb, 1)
                if t >= 3:
                    act.wait_ge(acc_ps, t - 2)
                act.copy(vext[:, t % 3, :, :], kv_bank[:, PAIR * M:2 * PAIR * M].rearrange("p (j o) -> p j o", j=PAIR)).then_inc(v_sb, 1)

            def gate_copy(t):
                act.wait_ge(xn2T_ps, t + 1)
                if t >= 1:
                    act.wait_ge(logits_ps, t)
                act.copy(xn2T[:], gate_bank[:].rearrange("p (c s) -> p c s", c=NCH)).then_inc(xn2T_sb, 1)

            def exps(t):
                if t >= 2:
                    act.wait_ge(turned_ps, PAIR * (t - 1))
                for h in range(2):
                    act.wait_ge(negmax_done, 2 * t + h + 1)
                    for c in range(2):
                        for j in range(PAIR):
                            q = (2 * h + c) * PAIR + j
                            ins = act.activation(probs[:, t % 2, 2 * h + c, j, :],
                                                 energy[:, h, (c * PAIR + j) * M:(c * PAIR + j + 1) * M], ACT.Exp,
                                                 bias=negmax[:, t % 2, q:q + 1],
                                                 accum_out=rowsum[:, t % 2, q:q + 1])
                    ins.then_inc(exp_done, 1)

            def turned_copy(t):
                for j in range(PAIR):
                    act.wait_ge(turned_ps, PAIR * t + j + 1)
                    if t >= 1:
                        act.wait_ge(acc_ps, t)
                    act.copy(probsT[:, j, :], turned[:, j, :]).then_inc(turned_sb, 1)

            def split_hi(e):
                act.wait_ge(w_in[e], 16)
                for c in range(PIECES):
                    act.copy(w_hi[:, e, c, :], w_raw[:, e % 2, c, :]).then_inc(hi_split, 1)

            kv_copy(0)
            kv_copy(1)
            act.wait_ge(be_dram, 16)
            exps(0)
            for t in range(NT):
                if t + 1 < NT:
                    exps(t + 1)
                turned_copy(t)
                if t + 2 < NT:
                    kv_copy(t + 2)
                if t >= 1:
                    gate_copy(t - 1)
                split_hi(t)
            gate_copy(NT - 1)

            for j in range(SLOT_TILES):
                act.wait_ge(xgT_ps, j + 1)
                if j >= 2:
                    act.wait_ge(y_ps, j - 1)
                act.copy(xgT_hi[:, j % 2, :], turned[:, j % 2, :]).then_inc(hi_turned, 1)
            for t in range(NT):
                act.wait_ge(fin_done, t + 1)
                act.dma_start(out_t[t], fin[:, t % 2, :]).then_inc(out_done[t % 2], 16)

        @block.vector
        def _(v):
            def chain(ins):
                tick[0] += 1
                ins.then_inc(dve, 1)
                v.wait_ge(dve, tick[0])

            v.wait_ge(be_in, 16)
            for k in range(3):
                v.tensor_copy(be_part[:, k, :], be_left[k % 2][:]).then_inc(be_parts, 1)
                if k < 2:
                    v.wait_ge(be_parts, k + 1)
                    chain(v.tensor_tensor(be_left[(k + 1) % 2][:], be_left[k % 2][:], be_part[:, k, :], ALU.subtract))

            v.wait_ge(zeroed, 7)
            v.wait_ge(set_ps, 1)
            for j in range(PAIR):
                r = slice(j * C, (j + 1) * C)
                v.tensor_scalar(at_diag[r, r], setup_bank[r, 0:C], C ** -0.5, None, ALU.mult).then_inc(set_sb, 1)
                v.tensor_copy(wv_diag[r, r], setup_bank[r, C:2 * C]).then_inc(set_sb, 1)
                v.tensor_copy(wskip_diag[r, r], setup_bank[r, 2 * C:3 * C]).then_inc(set_sb, 1)

            def norm1_stats(t):
                x_ready(v, t)
                chain(v.bn_stats(stats[:, t % 2, :], res[:, t, :]))
                chain(v.bn_aggr(mv[:, t % 2, :], stats[:, t % 2, :]))
                v.tensor_scalar(mv[:, t % 2, 1:2], mv[:, t % 2, 1:2], EPS, None, ALU.add).then_inc(mv_done, 1)

            def norm1(t):
                v.wait_ge(rstd_done, t + 1)
                if t >= 2:
                    v.wait_ge(turned_ps, PAIR * (t - 1))
                v.tensor_scalar(xn[:, t % 2, :], res[:, t, :], mv[:, t % 2, 0:1], rstd[:, t % 2, 0:1],
                                ALU.subtract, ALU.mult).then_inc(xn_done, 1)

            def row_max(t):
                if t >= 2:
                    v.wait_ge(exp_done, 2 * (t - 1))
                for h in range(2):
                    v.wait_ge(energy_ps, 2 * t + h + 1)
                    v.tensor_reduce(negmax[:, t % 2, 4 * h:4 * h + 4],
                                    energy[:, h, :].rearrange("p (q m) -> p q m", m=M), AX.X, ALU.max,
                                    negate=True).then_inc(negmax_done, 1)

            def normalise(t):
                v.wait_ge(exp_done, 2 * (t + 1))
                v.reciprocal(rinv[:, t % 2, :], rowsum[:, t % 2, :]).then_inc(rinv_done, 1)
                v.wait_ge(rinv_done, t + 1)
                for j in range(PAIR):
                    for c in range(NCH):
                        q = c * PAIR + j
                        ins = v.tensor_scalar(probs[:, t % 2, c, j, :], probs[:, t % 2, c, j, :],
                                              rinv[:, t % 2, q:q + 1], None, ALU.mult)
                    ins.then_inc(probs_done, 1)

            def residual(t):
                v.wait_ge(acc_ps, t + 1)
                v.tensor_tensor(res[:, t, :], acc[:], res[:, t, :], ALU.add).then_inc(acc_used, 1)
                v.wait_ge(acc_used, t + 1)
                chain(v.bn_stats(stats2[:, t % 2, :], res[:, t, :]))
                chain(v.bn_aggr(mv2[:, t % 2, :], stats2[:, t % 2, :]))
                v.tensor_scalar(mv2[:, t % 2, 1:2], mv2[:, t % 2, 1:2], EPS, None, ALU.add).then_inc(mv2_done, 1)

            def norm2(t):
                v.wait_ge(rstd2_done, t + 1)
                if t >= 2:
                    v.wait_ge(rows2_out[t % 2], 16 * (t // 2))
                    v.wait_ge(xn2T_ps, t - 1)
                v.tensor_scalar(xn2[:, t % 2, :], res[:, t, :], mv2[:, t % 2, 0:1], rstd2[:, t % 2, 0:1],
                                ALU.subtract, ALU.mult).then_inc(xn2_done, 1)

            def route(t):
                v.wait_ge(logits_ps, t + 1)
                v.wait_ge(gate_in, 32)
                v.tensor_tensor(logits[:], small_bank[:, 0:E], bg_rep[:], ALU.add).then_inc(logits_used, 1)
                v.wait_ge(logits_used, t + 1)
                chain(v.max(top8[:], logits[:]))
                chain(v.max_index(top_idx[:], top8[:], logits[:]))
                chain(v.tensor_copy(top_f[:], top_idx[:, 0:TOPK]))
                for k in range(TOPK):
                    ins = v.tensor_scalar(chosen[:, k, :, t], iota_e[:], top_f[:, k:k + 1], None, ALU.is_equal)
                chain(ins)

            v.wait_ge(consts, N_CONST)
            norm1_stats(0)
            norm1_stats(1)
            norm1(0)
            norm1(1)
            row_max(0)
            normalise(0)
            for t in range(NT):
                if t + 2 < NT:
                    norm1_stats(t + 2)
                if t >= 1:
                    residual(t - 1)
                if t + 1 < NT:
                    row_max(t + 1)
                if t + 2 < NT:
                    norm1(t + 2)
                if t >= 1:
                    norm2(t - 1)
                if t >= 2:
                    route(t - 2)
                if t + 1 < NT:
                    normalise(t + 1)
            residual(NT - 1)
            route(NT - 2)
            norm2(NT - 1)
            route(NT - 1)

            v.tensor_tensor(both[:], chosen[:, 0], chosen[:, 1], ALU.add).then_inc(both_done, 1)
            v.wait_ge(count_ps, 1)
            counts = setup_bank[:, 64:64 + E * NT]
            before = setup_bank[:, 0:E * NT].rearrange("p (e t) -> p e t", t=NT)
            chain(v.tensor_copy(tile_cnt[:].rearrange("p e t -> p (e t)"), counts))
            chain(v.tensor_tensor_scan(incl[:].rearrange("p e t -> p (e t)"), scan_keep[:],
                                       tile_cnt[:].rearrange("p e t -> p (e t)"), 0.0, ALU.mult, ALU.add))
            chain(v.tensor_tensor(over[:], incl[:, :, NT - 1:NT].to_broadcast([P, E, NT]),
                                  steps128[:].rearrange("p (a t) -> p a t", a=1).to_broadcast([P, E, NT]), ALU.is_gt))
            chain(v.tensor_reduce(ntile[:], over[:], AX.X, ALU.add))
            chain(v.tensor_tensor_scan(tile_end[:], scan_keep[:, 1:2].to_broadcast([P, E]), ntile[:], 0.0,
                                       ALU.mult, ALU.add))
            chain(v.tensor_tensor(past[:], iota_st[:].rearrange("p (s a) -> p s a", a=1).to_broadcast([P, ST, E]),
                                  tile_end[:].rearrange("p (a e) -> p a e", a=1).to_broadcast([P, ST, E]), ALU.is_ge))
            chain(v.tensor_reduce(exp_f[:], past[:], AX.X, ALU.add))
            v.tensor_scalar(exp_i[:], exp_f[:], float(E - 1), None, ALU.min).then_inc(exp_ids, 1)
            chain(v.tensor_tensor(slot0[:], incl[:], tile_cnt[:], ALU.subtract))
            chain(v.tensor_tensor(ntile[:], tile_end[:], ntile[:], ALU.subtract))
            chain(v.scalar_tensor_tensor(slot0[:], ntile[:].rearrange("p (e a) -> p e a", a=1).to_broadcast([P, E, NT]),
                                         float(P), slot0[:], ALU.mult, ALU.add))
            chain(v.tensor_tensor(slot_all[:], before, slot0[:], ALU.add))
            for k in range(TOPK):
                ins = v.tensor_tensor(slot_sel[:, k].rearrange("p t e -> p e t"), chosen[:, k], slot_all[:], ALU.mult)
            chain(ins)
            chain(v.tensor_reduce(slot_f[:], slot_sel[:], AX.X, ALU.add))
            chain(v.tensor_copy(slot_i[:], slot_f[:]))
            chain(v.tensor_scalar(lo_i[:], slot_i[:], P - 1, None, ALU.bitwise_and))
            chain(v.tensor_scalar(hi_i[:], slot_i[:], 7, None, ALU.arith_shift_right))
            v.tensor_copy(lo_f[:], lo_i[:]).then_inc(slots_known, 1)
            chain(v.tensor_copy(hi_f[:], hi_i[:]))
            chain(v.tensor_tensor(hi_eq[:], iota_st[:].rearrange("p (a s) -> p a s", a=1).to_broadcast([P, TOPK * NT, ST]),
                                  hi_f[:].rearrange("p k (t a) -> p (k t) a", a=1).to_broadcast([P, TOPK * NT, ST]), ALU.is_equal))
            v.tensor_tensor(hi_hot[:], hi_eq[:],
                            pair_no[:].rearrange("p k (t a) -> p (k t) a", a=1).to_broadcast([P, TOPK * NT, ST]),
                            ALU.mult).then_inc(hi_hot_done, 1)
            for t in range(NT):
                v.tensor_scalar(lo_hot[:, 0, t, :], iota_h[:], lo_f[:, 0, t:t + 1], None, ALU.is_equal).then_inc(lo_hot_dve, 1)
            v.wait_ge(pairs_ps, 1)
            chain(v.tensor_scalar(pair_f[:], small_bank[:, 0:ST], -1.0, None, ALU.add))
            chain(v.tensor_scalar(empty_f[:], pair_f[:], 0.0, float(SKIPPED), ALU.is_lt, ALU.mult))
            chain(v.tensor_tensor(scatter_i[:], pair_f[:], empty_f[:], ALU.add))
            chain(v.tensor_scalar(scat_f[:], pair_f[:], 0.0, None, ALU.max))
            chain(v.tensor_copy(pair_i[:], scat_f[:]))
            v.tensor_scalar(gather_i[:], pair_i[:], TOKENS - 1, None, ALU.bitwise_and).then_inc(slots_done, 1)

            def left_of(j):
                v.wait_ge(hi_turned, j + 1)
                if j >= 2:
                    v.wait_ge(y_ps, j - 1)
                v.tensor_tensor(xgT_lo[:, j % 2, :], turned[:, j % 2, :], xgT_hi[:, j % 2, :].bitcast(F32),
                                ALU.subtract).then_inc(lo_turned, 1)

            left_of(0)
            for j in range(SLOT_TILES):
                if j + 1 < SLOT_TILES:
                    left_of(j + 1)
                v.wait_ge(y_ps, j + 1)
                if j >= NG:
                    v.wait_ge(scattered[j % NG], 16 * (j // NG))
                v.tensor_scalar(ysb[:, j % NG, :], energy[:, j % 2, :], 0.0, 0.5, ALU.max, ALU.mult).then_inc(y_sb, 1)

            for t in range(NT):
                v.wait_ge(y_back[t % NY], 32 * (t // NY + 1))
                chain(v.tensor_tensor(y_in[:, t % NY, 0, :], y_in[:, t % NY, 0, :], y_in[:, t % NY, 1, :], ALU.add))
                if t >= 2:
                    v.wait_ge(out_done[t % 2], 16 * (t // 2))
                v.tensor_tensor(fin[:, t % 2, :], y_in[:, t % NY, 0, :], res[:, t, :], ALU.add).then_inc(fin_done, 1)

        @block.tensor
        def _(pe):
            pe.wait_ge(small_in, 16 * 8)
            pe.wait_ge(consts, N_CONST)
            dup = lambda i: w_small[:, i, :, :].rearrange("o r c -> o (r c)")
            pe.matmul(setup_bank[:, 0:C], dup(1), w_small[:, 0, 0, :], start=True, stop=True)
            pe.transpose(setup_bank[:, C:2 * C], dup(2), ident[0:C, 0:C])
            pe.transpose(setup_bank[:, 2 * C:3 * C], dup(3), ident[0:C, 0:C]).then_inc(set_ps, 1)

            def keys_values(t):
                if t == 0:
                    pe.wait_ge(ctx_in_s, 32)
                    pe.wait_ge(set_sb, 6)
                else:
                    pe.wait_ge(v_sb, t)
                pe.matmul(kv_bank[:, 0:PAIR * M], at_diag[:], ctx_diag[:, t, :, :].rearrange("p j m -> p (j m)"),
                          start=True, stop=True)
                for j in range(PAIR):
                    mm = pe.matmul(kv_bank[:, PAIR * M + j * P:PAIR * M + (j + 1) * P], ctx_diag[:, t, j, :],
                                   wv_diag[:], start=True, stop=True)
                mm.then_inc(kv_ps, 1)

            def energies(t):
                pe.wait_ge(xn_done, t + 1)
                pe.wait_ge(kk_sb, t + 1)
                for h in range(2):
                    if t >= 1:
                        pe.wait_ge(exp_done, 2 * (t - 1) + h + 1)
                    for c in range(2):
                        mm = pe.matmul(energy[:, h, c * PAIR * M:(c + 1) * PAIR * M],
                                       xn[:, t % 2, (2 * h + c) * P:(2 * h + c + 1) * P], kk[:, t % 2, :],
                                       start=True, stop=True)
                    mm.then_inc(energy_ps, 1)

            def attend(t):
                if t >= 1:
                    pe.wait_ge(acc_used, t)
                pe.matmul(acc[:], wskip_diag[:], xn[:, t % 2, :], start=True, stop=False)
                for j in range(PAIR):
                    pe.wait_ge(probs_done, PAIR * t + j + 1)
                    if t >= 1:
                        pe.wait_ge(turned_sb, PAIR * (t - 1) + j + 1)
                    for c in range(NCH):
                        mm = pe.transpose(turned[:, j, c * P:(c + 1) * P], probs[:, t % 2, c, j, :], ident[:])
                    mm.then_inc(turned_ps, 1)

            def values(t):
                pe.wait_ge(v_sb, t + 1)
                for j in range(PAIR):
                    pe.wait_ge(turned_sb, PAIR * t + j + 1)
                    mm = pe.matmul(acc[:], vext[:, t % 3, j, :], probsT[:, j, :], start=False, stop=(j == PAIR - 1))
                mm.then_inc(acc_ps, 1)

            def gate_turn(t):
                pe.wait_ge(xn2_done, t + 1)
                if t >= 1:
                    pe.wait_ge(xn2T_sb, t)
                for c in range(NCH):
                    mm = pe.transpose(gate_bank[:, c * P:(c + 1) * P], xn2[:, t % 2, c * P:(c + 1) * P], ident[:])
                mm.then_inc(xn2T_ps, 1)

            def gate_logits(t):
                pe.wait_ge(gate_in, 32)
                pe.wait_ge(xn2T_sb, t + 1)
                if t >= 1:
                    pe.wait_ge(logits_used, t)
                for c in range(NCH):
                    mm = pe.matmul(small_bank[:, 0:E], xn2T[:, c, :], w_gate[:, c, :], start=(c == 0), stop=(c == NCH - 1))
                mm.then_inc(logits_ps, 1)

            keys_values(0)
            keys_values(1)
            energies(0)
            for t in range(NT):
                if t + 1 < NT:
                    energies(t + 1)
                attend(t)
                if t + 2 < NT:
                    keys_values(t + 2)
                if t >= 1:
                    gate_turn(t - 1)
                values(t)
                if t >= 1:
                    gate_logits(t - 1)
            gate_turn(NT - 1)
            gate_logits(NT - 1)

            pe.wait_ge(both_done, 1)
            counted = both[:].rearrange("p e t -> p (e t)")
            pe.matmul(setup_bank[:, 0:E * NT], below_h[:], counted, start=True, stop=True)
            pe.matmul(setup_bank[:, 64:64 + E * NT], ones_h[:], counted, start=True, stop=True).then_inc(count_ps, 1)
            pe.wait_ge(hi_hot_done, 1)
            for t in range(NT):
                for k, ready in ((0, lo_hot_dve), (1, lo_hot_pool)):
                    pe.wait_ge(ready, t + 1)
                    mm = pe.matmul(small_bank[:, 0:ST], lo_hot[:, k, t, :], hi_hot[:, k * NT + t, :],
                                   start=(t == 0 and k == 0), stop=(t == NT - 1 and k == 1))
            mm.then_inc(pairs_ps, 1)

            def turn(j):
                pe.wait_ge(gathered[j % NG], 16 * (j // NG + 1))
                if j >= 2:
                    pe.wait_ge(lo_turned, j - 1)
                for c in range(NCH):
                    mm = pe.transpose(turned[:, j % 2, c * P:(c + 1) * P], xg[:, j % NG, c * P:(c + 1) * P], ident[:])
                mm.then_inc(xgT_ps, 1)

            pe.wait_ge(exp_ids, 1)
            pe.wait_ge(hi_split, PIECES * E)
            pe.wait_ge(lo_split, PIECES * E)
            pe.wait_ge(bias_in, 16)
            turn(0)
            for j in range(SLOT_TILES):
                e = pe.value_load(exp_i[0:1, j:j + 1], min_val=0, max_val=E - 1)
                if j >= 2:
                    pe.wait_ge(y_sb, j - 1)
                pe.matmul(energy[:, j % 2, :], ones3[:], bias3[:, bass.ds(e, 1), :].rearrange("k b h -> k (b h)"), start=True, stop=False)
                if j + 1 < SLOT_TILES:
                    turn(j + 1)
                pe.wait_ge(hi_turned, j + 1)
                for xp, wp in ((xgT_hi, w_hi), (xgT_hi, w_lo), (xgT_lo, w_hi)):
                    if xp is xgT_lo:
                        pe.wait_ge(lo_turned, j + 1)
                    for c in range(NCH):
                        mm = pe.matmul(energy[:, j % 2, :], xp[:, j % 2, c * P:(c + 1) * P],
                                       wp[:, bass.ds(e, 1), c, :].rearrange("p b h -> p (b h)"),
                                       start=False, stop=(xp is xgT_lo and c == NCH - 1))
                mm.then_inc(y_ps, 1)


_INS = ['x', 'ctx_1024', 'L0_xattn_Wq', 'L0_xattn_Wk', 'L0_xattn_Wv', 'L0_xattn_Wskip', 'L0_ffn_W_gate', 'L0_ffn_b_gate',
        'L0_ffn_W_e', 'L0_ffn_b_e']


def kernel(**inputs):
    import numpy as _np
    import concourse.bacc as _bacc
    from concourse import mybir as _mybir
    from concourse.bass_utils import run_bass_kernel_spmd as _run

    nc = _bacc.Bacc("TRN2", target_bir_lowering=False, num_devices=1)
    arrays, args = {}, []
    for name in _INS:
        a = _np.ascontiguousarray(inputs[name])
        arrays[f"in_{name}_dram"] = a
        args.append(nc.dram_tensor(f"in_{name}_dram", a.shape, _mybir.dt.from_np(a.dtype), kind="ExternalInput").ap())
    out = nc.dram_tensor("out_0_dram", inputs["x"].shape, _mybir.dt.float32, kind="ExternalOutput").ap()
    build_xattn_moe(nc, *args, out)
    r = _run(nc, [arrays], core_ids=[0])
    return r.results[0]["out_0_dram"]
```

```python
from contextlib import ExitStack

import concourse.bass as bass
from concourse import mybir

P = 128
ALU = mybir.AluOpType
ACT = mybir.ActivationFunctionType
F32 = mybir.dt.float32
F16 = mybir.dt.float16
I32 = mybir.dt.int32
BF16 = mybir.dt.bfloat16
F32R = mybir.dt.float32r
AX = mybir.AxisListType
EPS = 1e-5


def build_xattn_moe(nc, x, ctx_in, Wq, Wk, Wv, Wskip, W_gate, b_gate, W_e, b_e, out):
    B, C, D = x.shape
    M = ctx_in.shape[2]
    E, _, H = W_e.shape
    PAIR = P // C
    NT = B // PAIR
    NCH = D // P
    NQ = PAIR * NCH
    TOKENS = B * C
    TOPK = 2
    SLOT_TILES = TOKENS * TOPK // P + E - 1
    ST = SLOT_TILES + 1
    assert M == P and PAIR == 2 and D == H == 512 and NT == E == 8

    x_t = x.rearrange("(t j) c d -> t (j c) d", j=PAIR)
    ctx_t = ctx_in.rearrange("(t j) c m -> j c t m", j=PAIR)
    rows2 = nc.dram_tensor("normed_rows", (TOKENS, D), F32, kind="Internal").ap()
    MIN_TILES = TOKENS * TOPK // P

    PIECES = 4

    with ExitStack() as stack:
        def sb(name, shape, dt=F32):
            return stack.enter_context(nc.sbuf_tensor(name, shape, dt))

        def sem(name):
            return stack.enter_context(nc.semaphore(name))

        def over_at(name, host, start, shape, dt=F32):
            return nc.alloc_sbuf_tensor_at(name, shape, dt, offset=host_at[host] + start)

        host_at = {}

        def host(name, shape, dt=F32):
            host_at[name] = -(-nc.sbuf_base // 32) * 32
            return sb(name, shape, dt)

        res = host("res", [P, NT, D])
        b_rep = over_at("b_rep", "res", 0, [P, E, H])
        w_hi = sb("w_hi", [P, E, NCH, H], F32R)
        w_lo = host("w_lo", [P, E, NCH, H], F32R)
        w_raw = host("w_raw", [P, 2, NCH, H])
        ctx_diag = host("ctx_diag", [P, NT, PAIR, M])
        w_small = sb("w_small", [C, 4, 2, C])
        at_diag = sb("at_diag", [P, P])
        wv_diag = sb("wv_diag", [P, P])
        wskip_diag = sb("wskip_diag", [P, P])
        xn = host("xn", [P, 2, D])
        kk = sb("kk", [P, 2, PAIR * M])
        vext = sb("vext", [P, 3, PAIR, P])
        probs = host("probs", [P, 2, NCH, PAIR, M])
        probsT = host("probsT", [P, PAIR, D])
        stats = sb("stats", [P, 2, 6])
        mv = sb("mv", [P, 2, 2])
        rstd = sb("rstd", [P, 2, 1])
        stats2 = sb("stats2", [P, 2, 6])
        mv2 = sb("mv2", [P, 2, 2])
        rstd2 = sb("rstd2", [P, 2, 1])
        negmax = sb("negmax", [P, 2, NQ])
        rowsum = sb("rowsum", [P, 2, NQ])
        rinv = sb("rinv", [P, 2, NQ])
        xn2 = host("xn2", [P, 2, D])
        xn2T = sb("xn2T", [P, NCH, P])
        w_gate = sb("w_gate", [P, NCH, E])
        bg_rep = sb("bg_rep", [P, E])
        logits = sb("logits", [P, E])
        top8 = sb("top8", [P, 8])
        top_idx = sb("top_idx", [P, 8], mybir.dt.uint32)
        chosen = sb("chosen", [P, TOPK, E, NT], F16)
        both = sb("both", [P, E, NT], F16)
        ident = sb("ident", [P, P])
        power = sb("power", [P, 1])
        ones_h = sb("ones_h", [P, P], F16)
        below_h = sb("below_h", [P, P], F16)
        before_h = sb("before_h", [P, P], F16)
        iota_h = sb("iota_h", [P, P], F16)
        iota_e = sb("iota_e", [P, E])
        scan_keep = sb("scan_keep", [P, E * NT])
        steps128 = sb("steps128", [P, NT])
        iota_st = sb("iota_st", [P, ST])
        pair_no = sb("pair_no", [P, TOPK, NT])
        incl = sb("incl", [P, E, NT])
        over = sb("over", [P, E, NT])
        ntile = sb("ntile", [P, E])
        tile_end = sb("tile_end", [P, E])
        slot0 = sb("slot0", [P, E, NT])
        slot_all = sb("slot_all", [P, E, NT])
        slot_sel = sb("slot_sel", [P, TOPK, NT, E])
        slot_f = sb("slot_f", [P, TOPK, NT])
        slot_i = sb("slot_i", [P, TOPK, NT], I32)
        hi_i = sb("hi_i", [P, TOPK, NT], I32)
        lo_i = sb("lo_i", [P, TOPK, NT], I32)
        lo_hot = over_at("lo_hot", "w_raw", 0, [P, TOPK, NT, P], F16)
        hi_eq = over_at("hi_eq", "w_raw", 4096, [P, TOPK * NT, ST])
        hi_hot = over_at("hi_hot", "w_raw", 4096 + 1536, [P, TOPK * NT, ST], F16)
        past = over_at("past", "w_raw", 4096 + 2304, [P, ST, E])
        exp_i = sb("exp_i", [P, ST], I32)
        first_tile = sb("first_tile", [P, E])
        exp_f = sb("exp_f", [P, ST])
        n_used = sb("n_used", [P, 1], I32)
        pair_i = sb("pair_i", [P, ST], I32)
        token_f = sb("token_f", [P, ST])
        empty_f = sb("empty_f", [P, ST])
        junk_row = sb("junk_row", [P, 1])
        gather_i = sb("gather_i", [P, ST], I32)
        scatter_i = sb("scatter_i", [P, ST], I32)
        NG = 4
        xg = over_at("xg", "probs", 0, [P, NG, D])
        xgT_hi = over_at("xgT_hi", "xn", 0, [P, 2, D], F32R)
        xgT_lo = over_at("xgT_lo", "xn2", 0, [P, 2, D], F32R)
        ysb = over_at("ysb", "w_raw", 0, [P, NG, H])

        bank = [stack.enter_context(nc.psum_tensor(f"bank{i}", [P, 512], F32)) for i in range(4)]
        energy = stack.enter_context(nc.psum_tensor("energy", [P, 2, 512], F32))
        turned = stack.enter_context(nc.psum_tensor("turned", [P, PAIR, 512], F32))
        acc, gate_bank, kv_bank, small_bank = bank
        setup_bank = kv_bank

        x_in = [sem("x_in0"), sem("x_in1"), sem("x_in_rest")]
        ctx_in_s = sem("ctx_in_s")
        small_in = sem("small_in")
        gate_in = sem("gate_in")
        w_in = [sem(f"w_in{e}") for e in range(E)]
        consts = sem("consts")
        zeroed = sem("zeroed")
        set_ps = sem("set_ps")
        set_sb = sem("set_sb")
        mv_done = sem("mv_done")
        rstd_done = sem("rstd_done")
        xn_done = sem("xn_done")
        kv_ps = sem("kv_ps")
        kk_sb = sem("kk_sb")
        v_sb = sem("v_sb")
        energy_ps = sem("energy_ps")
        negmax_done = sem("negmax_done")
        exp_done = sem("exp_done")
        rinv_done = sem("rinv_done")
        probs_done = sem("probs_done")
        turned_ps = sem("turned_ps")
        turned_sb = sem("turned_sb")
        acc_ps = sem("acc_ps")
        acc_used = sem("acc_used")
        mv2_done = sem("mv2_done")
        rstd2_done = sem("rstd2_done")
        xn2_done = sem("xn2_done")
        rows2_out = [sem("rows2_out0"), sem("rows2_out1")]
        xn2T_ps = sem("xn2T_ps")
        xn2T_sb = sem("xn2T_sb")
        logits_ps = sem("logits_ps")
        logits_used = sem("logits_used")
        dve = sem("dve")
        both_done = sem("both_done")
        count_ps = sem("count_ps")
        pairs_ps = sem("pairs_ps")
        slots_done = sem("slots_done")
        gathered = [sem(f"gathered{i}") for i in range(NG)]
        xgT_ps = sem("xgT_ps")
        y_ps = sem("y_ps")
        y_sb = sem("y_sb")
        scattered = [sem(f"scattered{i}") for i in range(NG)]
        all_scattered = sem("all_scattered")
        scatter_ids = sem("scatter_ids")
        sums_in = sem("sums_in")
        ctx_zero = sem("ctx_zero")
        ctx_zero_pool = sem("ctx_zero_pool")
        n_used_done = sem("n_used_done")
        before_done = sem("before_done")
        bias_in = sem("bias_in")
        y_biased = sem("y_biased")
        hi_split = sem("hi_split")
        lo_split = sem("lo_split")
        slots_known = sem("slots_known")
        lo_hot_pool = sem("lo_hot_pool")
        lo_hot_dve = sem("lo_hot_dve")
        hi_hot_done = sem("hi_hot_done")
        hi_turned = sem("hi_turned")
        lo_turned = sem("lo_turned")

        N_CONST = 11
        POOL_HOTS = 3
        tick = [0]

        block = stack.enter_context(nc.Block())

        def if_used(eng, used, j, work):
            if j < MIN_TILES:
                work()
            else:
                with eng.If(used > j):
                    work()

        def x_ready(eng, t):
            eng.wait_ge(x_in[min(t, 2)], 16)

        @block.sync
        def _(sp):
            def store_rows(t):
                sp.wait_ge(acc_used, t + 1)
                sp.dma_start(out[t * P:(t + 1) * P, :], res[:, t, :]).then_inc(sums_in, 16)
                sp.wait_ge(xn2_done, t + 1)
                sp.dma_start(rows2[t * P:(t + 1) * P, :], xn2[:, t % 2, :]).then_inc(rows2_out[t % 2], 16)

            def load_bias(e):
                sp.dma_start(b_rep[:, e, :], b_e[e].rearrange("(a e) h -> a e h", a=1).to_broadcast([P, e.stop - e.start, H])).then_inc(bias_in, 16)

            for i, w in enumerate((Wq, Wk, Wv, Wskip)):
                sp.dma_start(w_small[:, i, :, :], w.rearrange("o (a c) -> o a c", a=1).to_broadcast([C, 2, C])).then_inc(small_in, 16)
            sp.wait_ge(ctx_zero_pool, 1)
            sp.wait_ge(ctx_zero, 1)
            for j in range(PAIR):
                sp.dma_start(ctx_diag[j * C:(j + 1) * C, :, j, :], ctx_t[j]).then_inc(ctx_in_s, 16)
            sp.dma_start(res[:, 2:NT, :], x_t[2:NT].rearrange("t p d -> p t d")).then_inc(x_in[2], 16)
            sp.dma_start(w_gate[:], W_gate.rearrange("(c p) e -> p c e", p=P)).then_inc(gate_in, 16)
            sp.dma_start(bg_rep[:], b_gate.rearrange("(a e) -> a e", a=1).to_broadcast([P, E])).then_inc(gate_in, 16)
            for e in range(E):
                if e >= 2:
                    sp.wait_ge(lo_split, PIECES * (e - 1))
                sp.dma_start(w_raw[:, e % 2, :, :], W_e[e].rearrange("(c p) h -> p c h", p=P)).then_inc(w_in[e], 16)
                if e >= 2:
                    store_rows(e - 2)
            for t in range(E - 2, NT):
                sp.wait_ge(sums_in, 16 * t)
                load_bias(slice(0, t) if t == E - 2 else slice(t - 1, t))
                store_rows(t)
            sp.wait_ge(sums_in, 16 * NT)
            load_bias(slice(NT - 1, NT))
            sp.wait_ge(all_scattered, 1)

        @block.gpsimd
        def _(pool):
            pool.memset(ctx_diag[C:P, :, 0, :], 0.0).then_inc(ctx_zero_pool, 1)
            pool.wait_ge(ctx_zero_pool, 1)
            pool.memset(at_diag[:], 0.0).then_inc(zeroed, 1)
            pool.memset(wv_diag[:], 0.0).then_inc(zeroed, 1)
            pool.memset(wskip_diag[:], 0.0).then_inc(zeroed, 1)
            pool.memset(power[:], -0.5).then_inc(consts, 1)
            pool.memset(ident[:], 0.0).then_inc(zeroed, 1)
            pool.memset(below_h[:], 1.0).then_inc(zeroed, 1)
            pool.memset(ones_h[:], 1.0).then_inc(consts, 1)
            pool.memset(scan_keep[:], 1.0).then_inc(zeroed, 1)
            pool.wait_ge(zeroed, 6)
            pool.affine_select(out=ident[:], in_=ident[:], compare_op=ALU.not_equal, fill=1.0, base=0,
                               pattern=[[-1, P]], channel_multiplier=1).then_inc(consts, 1)
            pool.affine_select(out=below_h[:], in_=below_h[:], compare_op=ALU.is_gt, fill=0.0, base=0,
                               pattern=[[1, P]], channel_multiplier=-1).then_inc(consts, 1)
            sk = scan_keep[:].rearrange("p (e t) -> p e t", t=NT)
            pool.affine_select(out=sk, in_=sk, compare_op=ALU.not_equal, fill=0.0, base=0,
                               pattern=[[0, E], [1, NT]], channel_multiplier=0).then_inc(consts, 1)
            pool.iota(iota_h[:], [[1, P]], base=0, channel_multiplier=0,
                      allow_small_or_imprecise_dtypes=True).then_inc(consts, 1)
            pool.iota(iota_e[:], [[1, E]], base=0, channel_multiplier=0,
                      allow_small_or_imprecise_dtypes=True).then_inc(consts, 1)
            pool.iota(steps128[:], [[P, NT]], base=0, channel_multiplier=0,
                      allow_small_or_imprecise_dtypes=True).then_inc(consts, 1)
            pool.iota(iota_st[:], [[1, ST]], base=0, channel_multiplier=0,
                      allow_small_or_imprecise_dtypes=True).then_inc(consts, 1)
            pool.iota(pair_no[:], [[TOKENS, TOPK], [P, NT]], base=1, channel_multiplier=1,
                      allow_small_or_imprecise_dtypes=True).then_inc(consts, 1)
            pool.iota(junk_row[:], [[0, 1]], base=TOKENS, channel_multiplier=1,
                      allow_small_or_imprecise_dtypes=True).then_inc(consts, 1)
            pool.wait_ge(consts, N_CONST)
            pool.tensor_tensor(before_h[:], below_h[:], ones_h[:], ALU.subtract).then_inc(before_done, 1)

            def root(mv_, rstd_, ready, done, t):
                pool.wait_ge(ready, t + 1)
                pool.tensor_tensor(rstd_[:, t % 2, :], mv_[:, t % 2, 1:2], power[:], ALU.pow).then_inc(done, 1)

            def split_lo(e):
                for c in range(PIECES):
                    pool.wait_ge(hi_split, PIECES * e + c + 1)
                    pool.tensor_tensor(w_lo[:, e, c, :], w_raw[:, e % 2, c, :], w_hi[:, e, c, :].bitcast(F32),
                                       ALU.subtract).then_inc(lo_split, 1)

            root(mv, rstd, mv_done, rstd_done, 0)
            root(mv, rstd, mv_done, rstd_done, 1)
            for t in range(NT):
                if t >= 1:
                    root(mv2, rstd2, mv2_done, rstd2_done, t - 1)
                if t + 2 < NT:
                    root(mv, rstd, mv_done, rstd_done, t + 2)
                if t == NT - 1:
                    root(mv2, rstd2, mv2_done, rstd2_done, t)
                split_lo(t)

            pool.wait_ge(slots_known, 1)
            for t in range(NT - POOL_HOTS, NT):
                pool.tensor_scalar(lo_hot[:, 1, t, :], iota_h[:], lo_i[:, 1, t:t + 1], None, ALU.is_equal).then_inc(lo_hot_pool, 1)
            pool.wait_ge(slots_done, 1)
            for i in range(2):
                pool.wait_ge(rows2_out[i], 16 * NT // 2)

            def gather(j):
                if j >= NG:
                    pool.wait_ge(xgT_ps, j - NG + 1)
                pool.indirect_dma_start(xg[:, j % NG, :], None, rows2,
                                        bass.IndirectOffsetOnAxis(gather_i[:, j:j + 1], 0)).then_inc(gathered[j % NG], 16)

            def added_before(j):
                for i in range(max(0, j - NG), j):
                    pool.wait_ge(scattered[i % NG], 16 * (i // NG + 1))

            def add_rows(j):
                pool.wait_ge(y_sb, j + 1)
                if j >= 1:
                    with pool.If(experts[j] > experts[j - 1]):
                        added_before(j)
                pool.indirect_dma_start(out, bass.IndirectOffsetOnAxis(scatter_i[:, j:j + 1], 0),
                                        ysb[:, j % NG, :], None, bounds_check=TOKENS + P - 1,
                                        oob_is_err=True, compute_op=ALU.add).then_inc(scattered[j % NG], 16)

            for j in range(NG):
                gather(j)
            pool.wait_ge(n_used_done, 1)
            used = pool.value_load(n_used[0:1, 0:1], min_val=MIN_TILES, max_val=SLOT_TILES)
            experts = [pool.value_load(exp_i[0:1, j:j + 1], min_val=0, max_val=E - 1) for j in range(SLOT_TILES)]
            pool.wait_ge(scatter_ids, 1)
            pool.wait_ge(sums_in, 16 * NT)
            for j in range(SLOT_TILES):
                if j + NG < SLOT_TILES:
                    if_used(pool, used, j + NG, lambda: gather(j + NG))
                if_used(pool, used, j, lambda: add_rows(j))
            for j in range(MIN_TILES, SLOT_TILES + 1):
                with pool.If(used == j):
                    added_before(j)
            pool.sem_inc(all_scattered, 1)

        @block.scalar
        def _(act):
            for t in range(2):
                act.dma_start(res[:, t, :], x_t[t]).then_inc(x_in[t], 16)

            def kv_copy(t):
                act.wait_ge(kv_ps, t + 1)
                if t >= 2:
                    act.wait_ge(energy_ps, 2 * (t - 1))
                act.copy(kk[:, t % 2, :], kv_bank[:, 0:PAIR * M]).then_inc(kk_sb, 1)
                if t >= 3:
                    act.wait_ge(acc_ps, t - 2)
                act.copy(vext[:, t % 3, :, :], kv_bank[:, PAIR * M:2 * PAIR * M].rearrange("p (j o) -> p j o", j=PAIR)).then_inc(v_sb, 1)

            def gate_copy(t):
                act.wait_ge(xn2T_ps, t + 1)
                if t >= 1:
                    act.wait_ge(logits_ps, t)
                act.copy(xn2T[:], gate_bank[:].rearrange("p (c s) -> p c s", c=NCH)).then_inc(xn2T_sb, 1)

            def exps(t):
                if t >= 2:
                    act.wait_ge(turned_ps, PAIR * (t - 1))
                for h in range(2):
                    act.wait_ge(negmax_done, 2 * t + h + 1)
                    for c in range(2):
                        for j in range(PAIR):
                            q = (2 * h + c) * PAIR + j
                            ins = act.activation(probs[:, t % 2, 2 * h + c, j, :],
                                                 energy[:, h, (c * PAIR + j) * M:(c * PAIR + j + 1) * M], ACT.Exp,
                                                 bias=negmax[:, t % 2, q:q + 1],
                                                 accum_out=rowsum[:, t % 2, q:q + 1])
                    ins.then_inc(exp_done, 1)

            def turned_copy(t):
                for j in range(PAIR):
                    act.wait_ge(turned_ps, PAIR * t + j + 1)
                    if t >= 1:
                        act.wait_ge(acc_ps, t)
                    act.copy(probsT[:, j, :], turned[:, j, :]).then_inc(turned_sb, 1)

            def split_hi(e):
                act.wait_ge(w_in[e], 16)
                for c in range(PIECES):
                    act.copy(w_hi[:, e, c, :], w_raw[:, e % 2, c, :]).then_inc(hi_split, 1)

            kv_copy(0)
            kv_copy(1)
            exps(0)
            for t in range(NT):
                if t + 1 < NT:
                    exps(t + 1)
                turned_copy(t)
                if t + 2 < NT:
                    kv_copy(t + 2)
                if t >= 1:
                    gate_copy(t - 1)
                split_hi(t)
            gate_copy(NT - 1)

            def high_part(j):
                act.wait_ge(xgT_ps, j + 1)
                if j >= 2:
                    act.wait_ge(y_ps, j - 1)
                act.copy(xgT_hi[:, j % 2, :], turned[:, j % 2, :]).then_inc(hi_turned, 1)

            act.wait_ge(n_used_done, 1)
            used = act.value_load(n_used[0:1, 0:1], min_val=MIN_TILES, max_val=SLOT_TILES)
            def mean_part(j):
                act.wait_ge(y_biased, j + 1)
                act.activation(ysb[:, j % NG, :], ysb[:, j % NG, :], ACT.Relu, scale=1.0 / TOPK).then_inc(y_sb, 1)

            high_part(0)
            for j in range(SLOT_TILES):
                if j + 1 < SLOT_TILES:
                    if_used(act, used, j + 1, lambda: high_part(j + 1))
                if_used(act, used, j, lambda: mean_part(j))

        @block.vector
        def _(v):
            def chain(ins):
                tick[0] += 1
                ins.then_inc(dve, 1)
                v.wait_ge(dve, tick[0])

            v.memset(ctx_diag[0:C, :, 1, :], 0.0).then_inc(ctx_zero, 1)

            def norm1_stats(t):
                x_ready(v, t)
                chain(v.bn_stats(stats[:, t % 2, :], res[:, t, :]))
                chain(v.bn_aggr(mv[:, t % 2, :], stats[:, t % 2, :]))
                v.tensor_scalar(mv[:, t % 2, 1:2], mv[:, t % 2, 1:2], EPS, None, ALU.add).then_inc(mv_done, 1)

            def norm1(t):
                v.wait_ge(rstd_done, t + 1)
                if t >= 2:
                    v.wait_ge(turned_ps, PAIR * (t - 1))
                v.tensor_scalar(xn[:, t % 2, :], res[:, t, :], mv[:, t % 2, 0:1], rstd[:, t % 2, 0:1],
                                ALU.subtract, ALU.mult).then_inc(xn_done, 1)

            def row_max(t):
                if t >= 2:
                    v.wait_ge(exp_done, 2 * (t - 1))
                for h in range(2):
                    v.wait_ge(energy_ps, 2 * t + h + 1)
                    v.tensor_reduce(negmax[:, t % 2, 4 * h:4 * h + 4],
                                    energy[:, h, :].rearrange("p (q m) -> p q m", m=M), AX.X, ALU.max,
                                    negate=True).then_inc(negmax_done, 1)

            def normalise(t):
                v.wait_ge(exp_done, 2 * (t + 1))
                v.reciprocal(rinv[:, t % 2, :], rowsum[:, t % 2, :]).then_inc(rinv_done, 1)
                v.wait_ge(rinv_done, t + 1)
                for j in range(PAIR):
                    for c in range(NCH):
                        q = c * PAIR + j
                        ins = v.tensor_scalar(probs[:, t % 2, c, j, :], probs[:, t % 2, c, j, :],
                                              rinv[:, t % 2, q:q + 1], None, ALU.mult)
                    ins.then_inc(probs_done, 1)

            def residual(t):
                v.wait_ge(acc_ps, t + 1)
                v.tensor_tensor(res[:, t, :], acc[:], res[:, t, :], ALU.add).then_inc(acc_used, 1)
                v.wait_ge(acc_used, t + 1)
                chain(v.bn_stats(stats2[:, t % 2, :], res[:, t, :]))
                chain(v.bn_aggr(mv2[:, t % 2, :], stats2[:, t % 2, :]))
                v.tensor_scalar(mv2[:, t % 2, 1:2], mv2[:, t % 2, 1:2], EPS, None, ALU.add).then_inc(mv2_done, 1)

            def norm2(t):
                v.wait_ge(rstd2_done, t + 1)
                if t >= 2:
                    v.wait_ge(rows2_out[t % 2], 16 * (t // 2))
                    v.wait_ge(xn2T_ps, t - 1)
                v.tensor_scalar(xn2[:, t % 2, :], res[:, t, :], mv2[:, t % 2, 0:1], rstd2[:, t % 2, 0:1],
                                ALU.subtract, ALU.mult).then_inc(xn2_done, 1)

            def route(t):
                v.wait_ge(logits_ps, t + 1)
                v.wait_ge(gate_in, 32)
                v.tensor_tensor(logits[:], small_bank[:, 0:E], bg_rep[:], ALU.add).then_inc(logits_used, 1)
                v.wait_ge(logits_used, t + 1)
                chain(v.max(top8[:], logits[:]))
                chain(v.max_index(top_idx[:], top8[:], logits[:]))
                for k in range(TOPK):
                    ins = v.tensor_scalar(chosen[:, k, :, t], iota_e[:], top_idx[:, k:k + 1], None, ALU.is_equal)
                chain(ins)

            def place_weights():
                v.wait_ge(zeroed, 6)
                v.wait_ge(set_ps, 1)
                for j in range(PAIR):
                    r = slice(j * C, (j + 1) * C)
                    v.tensor_scalar(at_diag[r, r], setup_bank[r, 0:C], C ** -0.5, None, ALU.mult).then_inc(set_sb, 1)
                    v.tensor_copy(wv_diag[r, r], setup_bank[r, C:2 * C]).then_inc(set_sb, 1)
                    v.tensor_copy(wskip_diag[r, r], setup_bank[r, 2 * C:3 * C]).then_inc(set_sb, 1)

            norm1_stats(0)
            place_weights()
            norm1_stats(1)
            v.wait_ge(consts, N_CONST)
            norm1(0)
            norm1(1)
            row_max(0)
            normalise(0)
            for t in range(NT):
                if t + 1 < NT:
                    row_max(t + 1)
                if t >= 1:
                    residual(t - 1)
                if t + 2 < NT:
                    norm1_stats(t + 2)
                if t >= 1:
                    norm2(t - 1)
                if t + 2 < NT:
                    norm1(t + 2)
                if t + 1 < NT:
                    normalise(t + 1)
                if t >= 2:
                    route(t - 2)
            residual(NT - 1)
            route(NT - 2)
            norm2(NT - 1)
            route(NT - 1)

            v.tensor_tensor(both[:], chosen[:, 0], chosen[:, 1], ALU.add).then_inc(both_done, 1)
            v.wait_ge(lo_split, PIECES * (E - 1))
            v.wait_ge(count_ps, 1)
            counts = setup_bank[:, 64:64 + E * NT]
            before = setup_bank[:, 0:E * NT].rearrange("p (e t) -> p e t", t=NT)
            chain(v.tensor_tensor_scan(incl[:].rearrange("p e t -> p (e t)"), scan_keep[:], counts, 0.0,
                                       ALU.mult, ALU.add))
            chain(v.tensor_tensor(over[:], incl[:, :, NT - 1:NT].to_broadcast([P, E, NT]),
                                  steps128[:].rearrange("p (a t) -> p a t", a=1).to_broadcast([P, E, NT]), ALU.is_gt))
            chain(v.tensor_reduce(ntile[:], over[:], AX.X, ALU.add))
            chain(v.tensor_tensor_scan(tile_end[:], scan_keep[:, 1:2].to_broadcast([P, E]), ntile[:], 0.0,
                                       ALU.mult, ALU.add))
            chain(v.tensor_tensor(first_tile[:], tile_end[:], ntile[:], ALU.subtract))
            chain(v.scalar_tensor_tensor(slot0[:], first_tile[:].rearrange("p (e a) -> p e a", a=1).to_broadcast([P, E, NT]),
                                         float(P), incl[:], ALU.mult, ALU.add))
            chain(v.tensor_tensor(slot_all[:], before, slot0[:], ALU.add))
            for k in range(TOPK):
                ins = v.tensor_tensor(slot_sel[:, k].rearrange("p t e -> p e t"), chosen[:, k], slot_all[:], ALU.mult)
            chain(ins)
            chain(v.tensor_reduce(slot_f[:], slot_sel[:], AX.X, ALU.add))
            chain(v.tensor_copy(slot_i[:], slot_f[:]))
            v.tensor_scalar(lo_i[:], slot_i[:], P - 1, None, ALU.bitwise_and).then_inc(slots_known, 1)
            chain(v.tensor_scalar(hi_i[:], slot_i[:], 7, None, ALU.arith_shift_right))
            chain(v.tensor_tensor(hi_eq[:], iota_st[:].rearrange("p (a s) -> p a s", a=1).to_broadcast([P, TOPK * NT, ST]),
                                  hi_i[:].rearrange("p k (t a) -> p (k t) a", a=1).to_broadcast([P, TOPK * NT, ST]), ALU.is_equal))
            v.tensor_tensor(hi_hot[:], hi_eq[:],
                            pair_no[:].rearrange("p k (t a) -> p (k t) a", a=1).to_broadcast([P, TOPK * NT, ST]),
                            ALU.mult).then_inc(hi_hot_done, 1)
            for t in range(NT):
                v.tensor_scalar(lo_hot[:, 0, t, :], iota_h[:], lo_i[:, 0, t:t + 1], None, ALU.is_equal).then_inc(lo_hot_dve, 1)
                if t < NT - POOL_HOTS:
                    v.tensor_scalar(lo_hot[:, 1, t, :], iota_h[:], lo_i[:, 1, t:t + 1], None, ALU.is_equal).then_inc(lo_hot_dve, 1)
            chain(v.tensor_copy(n_used[:], tile_end[:, E - 1:E]))
            chain(v.tensor_tensor(past[:], iota_st[:].rearrange("p (s a) -> p s a", a=1).to_broadcast([P, ST, E]),
                                  tile_end[:].rearrange("p (a e) -> p a e", a=1).to_broadcast([P, ST, E]), ALU.is_ge))
            chain(v.tensor_reduce(exp_f[:], past[:], AX.X, ALU.add))
            v.tensor_scalar(exp_i[:], exp_f[:], float(E - 1), None, ALU.min).then_inc(n_used_done, 1)
            v.wait_ge(pairs_ps, 1)
            chain(v.tensor_scalar(pair_i[:], small_bank[:, 0:ST], -1.0, 0.0, ALU.add, ALU.max))
            v.tensor_scalar(gather_i[:], pair_i[:], TOKENS - 1, None, ALU.bitwise_and).then_inc(slots_done, 1)
            chain(v.tensor_scalar(empty_f[:], small_bank[:, 0:ST], 0.0, junk_row[:, 0:1], ALU.is_equal, ALU.mult))
            v.wait_ge(slots_done, 1)
            v.tensor_tensor(scatter_i[:], empty_f[:], gather_i[:], ALU.add).then_inc(scatter_ids, 1)

            def left_of(j):
                v.wait_ge(hi_turned, j + 1)
                if j >= 2:
                    v.wait_ge(y_ps, j - 1)
                v.tensor_tensor(xgT_lo[:, j % 2, :], turned[:, j % 2, :], xgT_hi[:, j % 2, :].bitcast(F32),
                                ALU.subtract).then_inc(lo_turned, 1)

            def add_bias(j):
                e = v.value_load(exp_i[0:1, j:j + 1], min_val=0, max_val=E - 1)
                v.wait_ge(y_ps, j + 1)
                if j >= NG:
                    v.wait_ge(scattered[j % NG], 16 * (j // NG))
                v.tensor_tensor(ysb[:, j % NG, :], energy[:, j % 2, :],
                                b_rep[:, bass.ds(e, 1), :].rearrange("p b h -> p (b h)"), ALU.add).then_inc(y_biased, 1)

            v.wait_ge(n_used_done, 1)
            used = v.value_load(n_used[0:1, 0:1], min_val=MIN_TILES, max_val=SLOT_TILES)
            v.wait_ge(bias_in, 16 * 3)
            left_of(0)
            for j in range(SLOT_TILES):
                if j + 1 < SLOT_TILES:
                    if_used(v, used, j + 1, lambda: left_of(j + 1))
                if_used(v, used, j, lambda: add_bias(j))

        @block.tensor
        def _(pe):
            pe.wait_ge(small_in, 16 * 4)
            pe.wait_ge(consts, N_CONST)
            dup = lambda i: w_small[:, i, :, :].rearrange("o r c -> o (r c)")
            pe.matmul(setup_bank[:, 0:C], dup(1), w_small[:, 0, 0, :], start=True, stop=True)
            pe.transpose(setup_bank[:, C:2 * C], dup(2), ident[0:C, 0:C])
            pe.transpose(setup_bank[:, 2 * C:3 * C], dup(3), ident[0:C, 0:C]).then_inc(set_ps, 1)

            def keys_values(t):
                if t == 0:
                    pe.wait_ge(ctx_in_s, 32)
                    pe.wait_ge(set_sb, 6)
                else:
                    pe.wait_ge(v_sb, t)
                pe.matmul(kv_bank[:, 0:PAIR * M], at_diag[:], ctx_diag[:, t, :, :].rearrange("p j m -> p (j m)"),
                          start=True, stop=True)
                for j in range(PAIR):
                    mm = pe.matmul(kv_bank[:, PAIR * M + j * P:PAIR * M + (j + 1) * P], ctx_diag[:, t, j, :],
                                   wv_diag[:], start=True, stop=True)
                mm.then_inc(kv_ps, 1)

            def energies(t):
                pe.wait_ge(xn_done, t + 1)
                pe.wait_ge(kk_sb, t + 1)
                for h in range(2):
                    if t >= 1:
                        pe.wait_ge(exp_done, 2 * (t - 1) + h + 1)
                    for c in range(2):
                        mm = pe.matmul(energy[:, h, c * PAIR * M:(c + 1) * PAIR * M],
                                       xn[:, t % 2, (2 * h + c) * P:(2 * h + c + 1) * P], kk[:, t % 2, :],
                                       start=True, stop=True)
                    mm.then_inc(energy_ps, 1)

            def attend(t):
                if t >= 1:
                    pe.wait_ge(acc_used, t)
                pe.matmul(acc[:], wskip_diag[:], xn[:, t % 2, :], start=True, stop=False)
                for j in range(PAIR):
                    pe.wait_ge(probs_done, PAIR * t + j + 1)
                    if t >= 1:
                        pe.wait_ge(turned_sb, PAIR * (t - 1) + j + 1)
                    for c in range(NCH):
                        mm = pe.transpose(turned[:, j, c * P:(c + 1) * P], probs[:, t % 2, c, j, :], ident[:])
                    mm.then_inc(turned_ps, 1)

            def values(t):
                pe.wait_ge(v_sb, t + 1)
                for j in range(PAIR):
                    pe.wait_ge(turned_sb, PAIR * t + j + 1)
                    mm = pe.matmul(acc[:], vext[:, t % 3, j, :], probsT[:, j, :], start=False, stop=(j == PAIR - 1))
                mm.then_inc(acc_ps, 1)

            def gate_turn(t):
                pe.wait_ge(xn2_done, t + 1)
                if t >= 1:
                    pe.wait_ge(xn2T_sb, t)
                for c in range(NCH):
                    mm = pe.transpose(gate_bank[:, c * P:(c + 1) * P], xn2[:, t % 2, c * P:(c + 1) * P], ident[:])
                mm.then_inc(xn2T_ps, 1)

            def gate_logits(t):
                pe.wait_ge(gate_in, 32)
                pe.wait_ge(xn2T_sb, t + 1)
                if t >= 1:
                    pe.wait_ge(logits_used, t)
                for c in range(NCH):
                    mm = pe.matmul(small_bank[:, 0:E], xn2T[:, c, :], w_gate[:, c, :], start=(c == 0), stop=(c == NCH - 1))
                mm.then_inc(logits_ps, 1)

            keys_values(0)
            keys_values(1)
            energies(0)
            for t in range(NT):
                if t + 1 < NT:
                    energies(t + 1)
                if t >= 2:
                    gate_logits(t - 2)
                attend(t)
                if t + 2 < NT:
                    keys_values(t + 2)
                if t >= 1:
                    gate_turn(t - 1)
                values(t)
            gate_logits(NT - 2)
            gate_turn(NT - 1)
            gate_logits(NT - 1)

            pe.wait_ge(both_done, 1)
            pe.wait_ge(before_done, 1)
            counted = both[:].rearrange("p e t -> p (e t)")
            pe.matmul(setup_bank[:, 0:E * NT], before_h[:], counted, start=True, stop=True)
            pe.matmul(setup_bank[:, 64:64 + E * NT], ones_h[:], counted, start=True, stop=True).then_inc(count_ps, 1)
            pe.wait_ge(hi_hot_done, 1)
            for t in range(NT):
                for k in range(TOPK):
                    by_pool = max(0, t + 1 - (NT - POOL_HOTS))
                    if k == 1 and by_pool:
                        pe.wait_ge(lo_hot_pool, by_pool)
                    else:
                        pe.wait_ge(lo_hot_dve, TOPK * t + k + 1 - max(0, by_pool - 1))
                    mm = pe.matmul(small_bank[:, 0:ST], lo_hot[:, k, t, :], hi_hot[:, k * NT + t, :],
                                   start=(t == 0 and k == 0), stop=(t == NT - 1 and k == 1))
            mm.then_inc(pairs_ps, 1)

            def turn(j):
                pe.wait_ge(gathered[j % NG], 16 * (j // NG + 1))
                if j >= 2:
                    pe.wait_ge(lo_turned, j - 1)
                for c in range(NCH):
                    mm = pe.transpose(turned[:, j % 2, c * P:(c + 1) * P], xg[:, j % NG, c * P:(c + 1) * P], ident[:])
                mm.then_inc(xgT_ps, 1)

            pe.wait_ge(n_used_done, 1)
            used = pe.value_load(n_used[0:1, 0:1], min_val=MIN_TILES, max_val=SLOT_TILES)
            pe.wait_ge(hi_split, PIECES * E)
            pe.wait_ge(lo_split, PIECES * E)
            def multiply(j):
                e = pe.value_load(exp_i[0:1, j:j + 1], min_val=0, max_val=E - 1)
                if j >= 2:
                    pe.wait_ge(y_biased, j - 1)
                y = energy[:, j % 2, :]
                for xp, wp, ready in ((xgT_hi, w_hi, hi_turned), (xgT_hi, w_lo, hi_turned), (xgT_lo, w_hi, lo_turned)):
                    pe.wait_ge(ready, j + 1)
                    for c in range(NCH):
                        mm = pe.matmul(y, xp[:, j % 2, c * P:(c + 1) * P],
                                       wp[:, bass.ds(e, 1), c, :].rearrange("p b h -> p (b h)"),
                                       start=(wp is w_hi and xp is xgT_hi and c == 0), stop=(xp is xgT_lo and c == NCH - 1))
                mm.then_inc(y_ps, 1)

            turn(0)
            for j in range(SLOT_TILES):
                if j + 1 < SLOT_TILES:
                    if_used(pe, used, j + 1, lambda: turn(j + 1))
                if_used(pe, used, j, lambda: multiply(j))


_INS = ['x', 'ctx_1024', 'L0_xattn_Wq', 'L0_xattn_Wk', 'L0_xattn_Wv', 'L0_xattn_Wskip', 'L0_ffn_W_gate', 'L0_ffn_b_gate',
        'L0_ffn_W_e', 'L0_ffn_b_e']


def kernel(**inputs):
    import numpy as _np
    import concourse.bacc as _bacc
    from concourse import mybir as _mybir
    from concourse.bass_utils import run_bass_kernel_spmd as _run

    nc = _bacc.Bacc("TRN2", target_bir_lowering=False, num_devices=1)
    arrays, args = {}, []
    for name in _INS:
        a = _np.ascontiguousarray(inputs[name])
        arrays[f"in_{name}_dram"] = a
        args.append(nc.dram_tensor(f"in_{name}_dram", a.shape, _mybir.dt.from_np(a.dtype), kind="ExternalInput").ap())
    B, C, D = inputs["x"].shape
    out = nc.dram_tensor("out_0_dram", (B * C + P, D), _mybir.dt.float32, kind="ExternalOutput").ap()
    build_xattn_moe(nc, *args, out)
    r = _run(nc, [arrays], core_ids=[0])
    return r.results[0]["out_0_dram"][:B * C].reshape(B, C, D)
```

```python
from contextlib import ExitStack

import concourse.bass as bass
from concourse import mybir

P = 128
ALU = mybir.AluOpType
ACT = mybir.ActivationFunctionType
F32 = mybir.dt.float32
F16 = mybir.dt.float16
I32 = mybir.dt.int32
F32R = mybir.dt.float32r
AX = mybir.AxisListType
EPS = 1e-5


def build_xattn_moe(nc, x, ctx_in, Wq, Wk, Wv, Wskip, W_gate, b_gate, W_e, b_e, out):
    B, C, D = x.shape
    M = ctx_in.shape[2]
    E, _, H = W_e.shape
    PAIR = P // C
    NT = B // PAIR
    NCH = D // P
    NQ = PAIR * NCH
    TOKENS = B * C
    TOPK = 2
    MIN_TILES = TOKENS * TOPK // P
    SLOT_TILES = MIN_TILES + E - 1
    ST = SLOT_TILES + 1
    assert M == P and PAIR == 2 and D == H == 512 and NT == E == 8

    x_t = x.rearrange("(t j) c d -> t (j c) d", j=PAIR)
    ctx_t = ctx_in.rearrange("(t j) c m -> (j c) t m", j=PAIR)
    rows2 = nc.dram_tensor("normed_rows", (TOKENS, D), F32, kind="Internal").ap()
    PIECES = NCH
    NRAW = 3

    with ExitStack() as stack:
        def sb(name, shape, dt=F32):
            return stack.enter_context(nc.sbuf_tensor(name, shape, dt))

        def sem(name):
            return stack.enter_context(nc.semaphore(name))

        def over_at(name, host, start, shape, dt=F32):
            return nc.alloc_sbuf_tensor_at(name, shape, dt, offset=host_at[host] + start)

        host_at = {}

        def host(name, shape, dt=F32):
            host_at[name] = -(-nc.sbuf_base // 32) * 32
            return sb(name, shape, dt)

        res = host("res", [P, NT, D])
        b_rep = over_at("b_rep", "res", 0, [P, E, H])
        w_hi = sb("w_hi", [P, E, NCH, H], F32R)
        w_lo = host("w_lo", [P, E, NCH, H], F32R)
        w_raw = host("w_raw", [P, NRAW, NCH, H])
        ctx_sb = sb("ctx_sb", [P, NT, M])
        w_small = sb("w_small", [C, 4, 2, C])
        at_diag = sb("at_diag", [P, P])
        wv_diag = sb("wv_diag", [P, P])
        wskip_diag = sb("wskip_diag", [P, P])
        xn = host("xn", [P, 2, D])
        kk = host("kk", [P, 2, PAIR * M])
        vext = sb("vext", [P, 4, PAIR, P])
        probs = host("probs", [P, 2, NCH, PAIR, M])
        probsT = host("probsT", [P, PAIR, D])
        stats = sb("stats", [P, 2, 6])
        mv = sb("mv", [P, 2, 2])
        rstd = sb("rstd", [P, 2, 1])
        stats2 = sb("stats2", [P, 2, 6])
        mv2 = sb("mv2", [P, 2, 2])
        rstd2 = sb("rstd2", [P, 2, 1])
        negmax = sb("negmax", [P, 2, NQ])
        rowsum = sb("rowsum", [P, 2, NQ])
        rinv = sb("rinv", [P, 2, NQ])
        xn2 = host("xn2", [P, 2, D])
        xn2T = sb("xn2T", [P, NCH, P])
        w_gate = sb("w_gate", [P, NCH, E])
        bg_rep = sb("bg_rep", [P, E])
        logits = sb("logits", [P, E])
        top8 = sb("top8", [P, 8])
        top_idx = sb("top_idx", [P, 8], mybir.dt.uint32)
        chosen = sb("chosen", [P, TOPK, E, NT], F16)
        ident = sb("ident", [P, P])
        power = sb("power", [P, 1])
        idle_rows = over_at("idle_rows", "probsT", 0, [P, D], F16)
        ones_h = sb("ones_h", [P, P], F16)
        below_h = sb("below_h", [P, P], F16)
        before_h = sb("before_h", [P, P], F16)
        iota_h = sb("iota_h", [P, P], F16)
        iota_e = sb("iota_e", [P, E])
        scan_keep = sb("scan_keep", [P, E * NT])
        steps128 = sb("steps128", [P, NT])
        iota_st = sb("iota_st", [P, ST])
        token_no = sb("token_no", [P, TOPK, NT], F16)
        incl = over_at("incl", "kk", 0, [P, E, NT])
        over = over_at("over", "kk", 4 * E * NT, [P, E, NT])
        ntile = sb("ntile", [P, E])
        tile_start = sb("tile_start", [P, E + 1])
        slot0 = over_at("slot0", "kk", 8 * E * NT, [P, E, NT])
        slot_all = over_at("slot_all", "kk", 12 * E * NT, [P, E, NT])
        slot_sel = over_at("slot_sel", "kk", 16 * E * NT, [P, TOPK, NT, E])
        slot_f = sb("slot_f", [P, TOPK, NT])
        slot_i = sb("slot_i", [P, TOPK, NT], I32)
        hi_i = sb("hi_i", [P, TOPK, NT], I32)
        lo_i = sb("lo_i", [P, TOPK, NT], I32)
        lo_hot = over_at("lo_hot", "w_raw", 0, [P, TOPK, NT, P], F16)
        hi_eq = over_at("hi_eq", "w_raw", 4096, [P, TOPK * NT, ST], F16)
        hi_hot = over_at("hi_hot", "w_raw", 4096 + 1536, [P, TOPK * NT, ST], F16)
        past = over_at("past", "w_raw", 4096 + 2304, [P, ST, E])
        exp_i = sb("exp_i", [P, ST], I32)
        exp_f = sb("exp_f", [P, ST])
        n_used = sb("n_used", [P, 1], I32)
        empty_f = sb("empty_f", [P, ST])
        junk_row = sb("junk_row", [P, 1])
        gather_i = sb("gather_i", [P, ST], I32)
        scatter_i = sb("scatter_i", [P, ST], I32)
        NG = 4
        xg = over_at("xg", "probs", 0, [P, NG, D])
        xgT_hi = over_at("xgT_hi", "xn", 0, [P, 2, D], F32R)
        xgT_lo = over_at("xgT_lo", "xn2", 0, [P, 2, D], F32R)
        ysb = over_at("ysb", "w_raw", 0, [P, NG, H])

        bank = [stack.enter_context(nc.psum_tensor(f"bank{i}", [P, 512], F32)) for i in range(4)]
        energy = stack.enter_context(nc.psum_tensor("energy", [P, 2, 512], F32))
        turned = stack.enter_context(nc.psum_tensor("turned", [P, PAIR, 512], F32))
        acc, gate_bank, kv_bank, small_bank = bank
        setup_bank = kv_bank

        x_loaded = [sem("x_loaded0"), sem("x_loaded1"), sem("x_loaded_rest")]
        ctx_loaded = sem("ctx_loaded")
        small_loaded = sem("small_loaded")
        gate_loaded = sem("gate_loaded")
        w_loaded = [sem(f"w_loaded{e}") for e in range(E)]
        bias_loaded = sem("bias_loaded")
        residual_out = sem("residual_out")
        last_residual_out = sem("last_residual_out")
        rows2_out = [sem("rows2_out0"), sem("rows2_out1")]
        gathered = [sem(f"gathered{i}") for i in range(NG)]
        scattered = [sem(f"scattered{i}") for i in range(NG)]
        consts = sem("consts")
        zeroed = sem("zeroed")
        before_done = sem("before_done")
        kk_zero = sem("kk_zero")
        vext_zero = sem("vext_zero")
        idle_done = sem("idle_done")
        set_ps = sem("set_ps")
        set_sb = sem("set_sb")
        stats_done = sem("stats_done")
        aggr_done = sem("aggr_done")
        mv_done = sem("mv_done")
        rstd_done = sem("rstd_done")
        xn_done = sem("xn_done")
        kv_ps = sem("kv_ps")
        kk_sb = sem("kk_sb")
        v_sb = sem("v_sb")
        energy_ps = sem("energy_ps")
        negmax_done = sem("negmax_done")
        exp_done = sem("exp_done")
        rinv_done = sem("rinv_done")
        probs_done = sem("probs_done")
        turned_ps = sem("turned_ps")
        turned_sb = sem("turned_sb")
        skip_ps = sem("skip_ps")
        acc_ps = sem("acc_ps")
        acc_used = sem("acc_used")
        stats2_done = sem("stats2_done")
        aggr2_done = sem("aggr2_done")
        mv2_done = sem("mv2_done")
        rstd2_done = sem("rstd2_done")
        xn2_done = sem("xn2_done")
        xn2T_ps = sem("xn2T_ps")
        xn2T_sb = sem("xn2T_sb")
        logits_ps = sem("logits_ps")
        logits_used = sem("logits_used")
        top_done = sem("top_done")
        index_done = sem("index_done")
        choice_done = sem("choice_done")
        hi_split = sem("hi_split")
        lo_split = sem("lo_split")
        vector_step = sem("vector_step")
        count_ps = sem("count_ps")
        slots_known = sem("slots_known")
        hi_eq_done = sem("hi_eq_done")
        hi_hot_done = sem("hi_hot_done")
        lo_hot_dve = sem("lo_hot_dve")
        lo_hot_pool = sem("lo_hot_pool")
        slot_tokens_ps = sem("slot_tokens_ps")
        slots_done = sem("slots_done")
        scatter_ids = sem("scatter_ids")
        n_used_done = sem("n_used_done")
        xgT_ps = sem("xgT_ps")
        hi_turned = sem("hi_turned")
        lo_turned = sem("lo_turned")
        y_ps = sem("y_ps")
        y_biased = sem("y_biased")
        y_sb = sem("y_sb")
        all_scattered = sem("all_scattered")

        N_CONST = 12
        POOL_HOTS = 2
        START_IDLE, SETUP_IDLE, GATHER_IDLE = 12, 3, 8
        steps = [0]

        block = stack.enter_context(nc.Block())

        def if_used(eng, used, j, work):
            if j < MIN_TILES:
                work()
            else:
                with eng.If(used > j):
                    work()

        def kv_copy(eng, copy, t):
            eng.wait_ge(kv_ps, t + 1)
            if t >= 2:
                eng.wait_ge(energy_ps, 2 * (t - 1))
            if t < 2:
                eng.wait_ge(kk_zero, 1)
            for j in range(PAIR):
                copy(kk[j * C:(j + 1) * C, t % 2, j * M:(j + 1) * M], kv_bank[j * C:(j + 1) * C, 0:M]).then_inc(kk_sb, 1)
            if t >= 4:
                eng.wait_ge(acc_ps, t - 3)
            else:
                eng.wait_ge(vext_zero, 1)
            copy(vext[:, t % 4, :, :].rearrange("p j (h c) -> p (j h) c", c=C)[:, 0:2 * PAIR:2 * PAIR - 1, :],
                 kv_bank[:, M:M + P].rearrange("p (j c) -> p j c", c=C)).then_inc(v_sb, 1)

        def x_ready(eng, t):
            eng.wait_ge(x_loaded[min(t, 2)], 16)

        @block.sync
        def _(sp):
            def store_rows(t):
                sp.wait_ge(acc_used, t + 1)
                sp.dma_start(out[t * P:(t + 1) * P, :], res[:, t, :]).then_inc(residual_out if t < NT - 2 else last_residual_out, 16)
                sp.wait_ge(xn2_done, t + 1)
                sp.dma_start(rows2[t * P:(t + 1) * P, :], xn2[:, t % 2, :]).then_inc(rows2_out[t % 2], 16)

            def load_bias(e):
                sp.dma_start(b_rep[:, e, :], b_e[e].rearrange("(a e) h -> a e h", a=1).to_broadcast([P, e.stop - e.start, H])).then_inc(bias_loaded, 16)

            for i, w in enumerate((Wq, Wk, Wv, Wskip)):
                sp.dma_start(w_small[:, i, :, :], w.rearrange("o (a c) -> o a c", a=1).to_broadcast([C, 2, C])).then_inc(small_loaded, 16)
            sp.dma_start(ctx_sb[:], ctx_t).then_inc(ctx_loaded, 16)
            sp.dma_start(res[:, 2:NT, :], x_t[2:NT].rearrange("t p d -> p t d")).then_inc(x_loaded[2], 16)
            sp.dma_start(w_gate[:], W_gate.rearrange("(c p) e -> p c e", p=P)).then_inc(gate_loaded, 16)
            sp.dma_start(bg_rep[:], b_gate.rearrange("(a e) -> a e", a=1).to_broadcast([P, E])).then_inc(gate_loaded, 16)
            for e in range(E):
                if e >= NRAW:
                    store_rows(e - NRAW)
                    sp.wait_ge(lo_split, PIECES * (e - NRAW + 1))
                sp.dma_start(w_raw[:, e % NRAW, :, :], W_e[e].rearrange("(c p) h -> p c h", p=P)).then_inc(w_loaded[e], 16)
            for t in range(E - NRAW, NT - 1):
                store_rows(t)
            sp.wait_ge(residual_out, 16 * (NT - 2))
            load_bias(slice(0, NT - 2))
            store_rows(NT - 1)
            sp.wait_ge(last_residual_out, 16 * 2)
            load_bias(slice(NT - 2, NT))
            sp.wait_ge(all_scattered, 1)

        @block.gpsimd
        def _(pool):
            pool.memset(at_diag[:], 0.0).then_inc(zeroed, 1)
            pool.memset(wv_diag[:], 0.0).then_inc(zeroed, 1)
            pool.memset(wskip_diag[:], 0.0).then_inc(zeroed, 1)
            pool.memset(power[:], -0.5).then_inc(consts, 1)
            pool.memset(tile_start[:, 0:1], 0.0).then_inc(consts, 1)
            pool.memset(ident[:], 0.0).then_inc(zeroed, 1)
            pool.memset(below_h[:], 1.0).then_inc(zeroed, 1)
            pool.memset(ones_h[:], 1.0).then_inc(consts, 1)
            pool.memset(scan_keep[:], 1.0).then_inc(zeroed, 1)
            pool.wait_ge(zeroed, 6)
            pool.affine_select(out=ident[:], in_=ident[:], compare_op=ALU.not_equal, fill=1.0, base=0,
                               pattern=[[-1, P]], channel_multiplier=1).then_inc(consts, 1)
            pool.affine_select(out=below_h[:], in_=below_h[:], compare_op=ALU.is_gt, fill=0.0, base=0,
                               pattern=[[1, P]], channel_multiplier=-1).then_inc(consts, 1)
            sk = scan_keep[:].rearrange("p (e t) -> p e t", t=NT)
            pool.affine_select(out=sk, in_=sk, compare_op=ALU.not_equal, fill=0.0, base=0,
                               pattern=[[0, E], [1, NT]], channel_multiplier=0).then_inc(consts, 1)
            pool.iota(iota_h[:], [[1, P]], base=0, channel_multiplier=0,
                      allow_small_or_imprecise_dtypes=True).then_inc(consts, 1)
            pool.iota(iota_e[:], [[1, E]], base=0, channel_multiplier=0,
                      allow_small_or_imprecise_dtypes=True).then_inc(consts, 1)
            pool.iota(steps128[:], [[P, NT]], base=0, channel_multiplier=0,
                      allow_small_or_imprecise_dtypes=True).then_inc(consts, 1)
            pool.iota(iota_st[:], [[1, ST]], base=0, channel_multiplier=0,
                      allow_small_or_imprecise_dtypes=True).then_inc(consts, 1)
            pool.iota(token_no[:], [[0, TOPK], [P, NT]], base=1, channel_multiplier=1,
                      allow_small_or_imprecise_dtypes=True).then_inc(consts, 1)
            pool.iota(junk_row[:], [[0, 1]], base=TOKENS, channel_multiplier=1,
                      allow_small_or_imprecise_dtypes=True).then_inc(consts, 1)
            pool.wait_ge(consts, N_CONST)
            pool.tensor_tensor(before_h[:], below_h[:], ones_h[:], ALU.subtract).then_inc(before_done, 1)

            def root(mv_, rstd_, ready, done, t):
                pool.wait_ge(ready, t + 1)
                pool.tensor_tensor(rstd_[:, t % 2, :], mv_[:, t % 2, 1:2], power[:], ALU.pow).then_inc(done, 1)

            def split_lo(e, pieces=range(PIECES)):
                for c in pieces:
                    pool.wait_ge(hi_split, PIECES * e + c + 1)
                    pool.tensor_tensor(w_lo[:, e, c, :], w_raw[:, e % NRAW, c, :], w_hi[:, e, c, :].bitcast(F32),
                                       ALU.subtract).then_inc(lo_split, 1)

            root(mv, rstd, mv_done, rstd_done, 0)
            root(mv, rstd, mv_done, rstd_done, 1)
            for t in range(NT):
                if t + 2 < NT:
                    root(mv, rstd, mv_done, rstd_done, t + 2)
                if t >= 1:
                    root(mv2, rstd2, mv2_done, rstd2_done, t - 1)
                if 1 <= t < NT - 1:
                    split_lo(t - 1)
            split_lo(NT - 2, range(PIECES // 2))
            root(mv2, rstd2, mv2_done, rstd2_done, NT - 1)
            split_lo(NT - 2, range(PIECES // 2, PIECES))
            split_lo(NT - 1)

            pool.wait_ge(slots_known, 1)
            pool.wait_ge(hi_eq_done, 1)
            pool.tensor_tensor(hi_hot[:], hi_eq[:],
                               token_no[:].rearrange("p k (t a) -> p (k t) a", a=1).to_broadcast([P, TOPK * NT, ST]),
                               ALU.mult).then_inc(hi_hot_done, 1)
            for t in range(NT - POOL_HOTS, NT):
                pool.tensor_scalar(lo_hot[:, 1, t, :], iota_h[:], lo_i[:, 1, t:t + 1], None, ALU.is_equal).then_inc(lo_hot_pool, 1)
            pool.wait_ge(slots_done, 1)
            for i in range(2):
                pool.wait_ge(rows2_out[i], 16 * NT // 2)

            def gather(j):
                if j >= NG:
                    pool.wait_ge(xgT_ps, j - NG + 1)
                pool.indirect_dma_start(xg[:, j % NG, :], None, rows2,
                                        bass.IndirectOffsetOnAxis(gather_i[:, j:j + 1], 0)).then_inc(gathered[j % NG], 16)

            def added_before(j):
                for i in range(max(0, j - NG), j):
                    pool.wait_ge(scattered[i % NG], 16 * (i // NG + 1))

            experts = []

            def add_rows(j):
                pool.wait_ge(y_sb, j + 1)
                if j >= 1:
                    with pool.If(experts[j] > experts[j - 1]):
                        added_before(j)
                pool.indirect_dma_start(out, bass.IndirectOffsetOnAxis(scatter_i[:, j:j + 1], 0),
                                        ysb[:, j % NG, :], None, bounds_check=TOKENS + P - 1,
                                        oob_is_err=True, compute_op=ALU.add).then_inc(scattered[j % NG], 16)

            for j in range(NG):
                gather(j)
            pool.wait_ge(n_used_done, 1)
            used = pool.value_load(n_used[0:1, 0:1], min_val=MIN_TILES, max_val=SLOT_TILES)
            pool.wait_ge(scatter_ids, 1)
            pool.wait_ge(residual_out, 16 * (NT - 2))
            pool.wait_ge(last_residual_out, 16 * 2)
            for j in range(SLOT_TILES):
                if j + NG < SLOT_TILES:
                    if_used(pool, used, j + NG, lambda: gather(j + NG))
                experts.append(pool.value_load(exp_i[0:1, j:j + 1], min_val=0, max_val=E - 1))
                if_used(pool, used, j, lambda: add_rows(j))
            for j in range(MIN_TILES, SLOT_TILES + 1):
                with pool.If(used == j):
                    added_before(j)
            pool.sem_inc(all_scattered, 1)

        @block.scalar
        def _(act):
            for t in range(2):
                act.dma_start(res[:, t, :], x_t[t]).then_inc(x_loaded[t], 16)

            def gate_copy(t):
                act.wait_ge(xn2T_ps, t + 1)
                if t >= 1:
                    act.wait_ge(logits_ps, t)
                act.copy(xn2T[:], gate_bank[:].rearrange("p (c s) -> p c s", c=NCH)).then_inc(xn2T_sb, 1)

            def exps(t):
                if t >= 2:
                    act.wait_ge(turned_ps, PAIR * (t - 1))
                for h in range(2):
                    act.wait_ge(negmax_done, 2 * t + h + 1)
                    for c in range(2):
                        for j in range(PAIR):
                            q = (2 * h + c) * PAIR + j
                            ins = act.activation(probs[:, t % 2, 2 * h + c, j, :],
                                                 energy[:, h, (c * PAIR + j) * M:(c * PAIR + j + 1) * M], ACT.Exp,
                                                 bias=negmax[:, t % 2, q:q + 1],
                                                 accum_out=rowsum[:, t % 2, q:q + 1])
                    ins.then_inc(exp_done, 1)

            def turned_copy(t):
                for j in range(PAIR):
                    act.wait_ge(turned_ps, PAIR * t + j + 1)
                    if t >= 1:
                        act.wait_ge(acc_ps, t)
                    act.copy(probsT[:, j, :], turned[:, j, :]).then_inc(turned_sb, 1)

            def split_hi(e):
                act.wait_ge(w_loaded[e], 16)
                for c in range(PIECES):
                    act.copy(w_hi[:, e, c, :], w_raw[:, e % NRAW, c, :]).then_inc(hi_split, 1)

            kv_copy(act, act.copy, 0)
            exps(0)
            kv_copy(act, act.copy, 2)
            exps(1)
            for t in range(NT):
                if 2 <= t + 1 < NT:
                    exps(t + 1)
                turned_copy(t)
                if t + 3 < NT:
                    kv_copy(act, act.copy, t + 3)
                if t >= 2:
                    gate_copy(t - 2)
                if t < NT - 1:
                    split_hi(t)
            gate_copy(NT - 2)
            split_hi(NT - 1)
            gate_copy(NT - 1)

            def high_part(j):
                act.wait_ge(xgT_ps, j + 1)
                if j >= 2:
                    act.wait_ge(y_ps, j - 1)
                act.copy(xgT_hi[:, j % 2, :], turned[:, j % 2, :]).then_inc(hi_turned, 1)

            act.wait_ge(n_used_done, 1)
            used = act.value_load(n_used[0:1, 0:1], min_val=MIN_TILES, max_val=SLOT_TILES)
            def mean_part(j):
                act.wait_ge(y_biased, j + 1)
                act.activation(ysb[:, j % NG, :], ysb[:, j % NG, :], ACT.Relu, scale=1.0 / TOPK).then_inc(y_sb, 1)

            high_part(0)
            for j in range(SLOT_TILES):
                if j + 1 < SLOT_TILES:
                    if_used(act, used, j + 1, lambda: high_part(j + 1))
                if_used(act, used, j, lambda: mean_part(j))

        @block.vector
        def _(v):
            def chain(ins):
                steps[0] += 1
                ins.then_inc(vector_step, 1)
                v.wait_ge(vector_step, steps[0])

            v.memset(idle_rows[:], 0.0).then_inc(idle_done, 1)
            v.memset(kk[:], 0.0).then_inc(kk_zero, 1)
            v.memset(vext[:], 0.0).then_inc(vext_zero, 1)

            def stats1(t):
                x_ready(v, t)
                v.bn_stats(stats[:, t % 2, :], res[:, t, :]).then_inc(stats_done, 1)

            def mean_var1(t):
                v.wait_ge(stats_done, t + 1)
                v.bn_aggr(mv[:, t % 2, :], stats[:, t % 2, :]).then_inc(aggr_done, 1)

            def add_eps1(t):
                v.wait_ge(aggr_done, t + 1)
                v.tensor_scalar(mv[:, t % 2, 1:2], mv[:, t % 2, 1:2], EPS, None, ALU.add).then_inc(mv_done, 1)

            def norm1(t):
                v.wait_ge(rstd_done, t + 1)
                if t >= 2:
                    v.wait_ge(skip_ps, t - 1)
                v.tensor_scalar(xn[:, t % 2, :], res[:, t, :], mv[:, t % 2, 0:1], rstd[:, t % 2, 0:1],
                                ALU.subtract, ALU.mult).then_inc(xn_done, 1)

            def row_max(t, h):
                if t >= 2:
                    v.wait_ge(exp_done, 2 * (t - 1))
                v.wait_ge(energy_ps, 2 * t + h + 1)
                v.tensor_reduce(negmax[:, t % 2, 4 * h:4 * h + 4],
                                energy[:, h, :].rearrange("p (q m) -> p q m", m=M), AX.X, ALU.max,
                                negate=True).then_inc(negmax_done, 1)

            def normalise(t):
                v.wait_ge(exp_done, 2 * (t + 1))
                v.reciprocal(rinv[:, t % 2, :], rowsum[:, t % 2, :]).then_inc(rinv_done, 1)
                v.wait_ge(rinv_done, t + 1)
                for j in range(PAIR):
                    rows = probs[:, t % 2, :, j, :]
                    v.tensor_tensor(rows, rows, rinv[:, t % 2, j::PAIR].rearrange("p (c a) -> p c a", a=1).to_broadcast([P, NCH, M]),
                                    ALU.mult).then_inc(probs_done, 1)

            def residual(t):
                v.wait_ge(acc_ps, t + 1)
                v.tensor_tensor(res[:, t, :], acc[:], res[:, t, :], ALU.add).then_inc(acc_used, 1)

            def stats_2(t):
                v.wait_ge(acc_used, t + 1)
                v.bn_stats(stats2[:, t % 2, :], res[:, t, :]).then_inc(stats2_done, 1)

            def mean_var2(t):
                v.wait_ge(stats2_done, t + 1)
                v.bn_aggr(mv2[:, t % 2, :], stats2[:, t % 2, :]).then_inc(aggr2_done, 1)

            def add_eps2(t):
                v.wait_ge(aggr2_done, t + 1)
                v.tensor_scalar(mv2[:, t % 2, 1:2], mv2[:, t % 2, 1:2], EPS, None, ALU.add).then_inc(mv2_done, 1)

            def norm2(t):
                v.wait_ge(rstd2_done, t + 1)
                if t >= 2:
                    v.wait_ge(rows2_out[t % 2], 16 * (t // 2))
                    v.wait_ge(xn2T_ps, t - 1)
                v.tensor_scalar(xn2[:, t % 2, :], res[:, t, :], mv2[:, t % 2, 0:1], rstd2[:, t % 2, 0:1],
                                ALU.subtract, ALU.mult).then_inc(xn2_done, 1)

            def add_gate_bias(t):
                v.wait_ge(logits_ps, t + 1)
                v.wait_ge(gate_loaded, 32)
                v.tensor_tensor(logits[:], small_bank[:, 0:E], bg_rep[:], ALU.add).then_inc(logits_used, 1)

            def top(t):
                v.wait_ge(logits_used, t + 1)
                v.max(top8[:], logits[:]).then_inc(top_done, 1)

            def top_index(t):
                v.wait_ge(top_done, t + 1)
                v.max_index(top_idx[:], top8[:], logits[:]).then_inc(index_done, 1)

            def choose(t):
                v.wait_ge(index_done, t + 1)
                for k in range(TOPK):
                    v.tensor_scalar(chosen[:, k, :, t], iota_e[:], top_idx[:, k:k + 1], None, ALU.is_equal).then_inc(choice_done, 1)

            def route(t):
                add_gate_bias(t)
                top(t)
                top_index(t)
                choose(t)

            def place_weights():
                v.wait_ge(zeroed, 6)
                v.wait_ge(set_ps, 1)
                for j in range(PAIR):
                    r = slice(j * C, (j + 1) * C)
                    v.tensor_scalar(at_diag[r, r], setup_bank[r, 0:C], C ** -0.5, None, ALU.mult).then_inc(set_sb, 1)
                    v.tensor_copy(wv_diag[r, r], setup_bank[r, C:2 * C]).then_inc(set_sb, 1)
                    v.tensor_copy(wskip_diag[r, r], setup_bank[r, 2 * C:3 * C]).then_inc(set_sb, 1)

            stats1(0)
            mean_var1(0)
            add_eps1(0)
            place_weights()
            stats1(1)
            mean_var1(1)
            add_eps1(1)
            v.wait_ge(consts, N_CONST)
            norm1(0)
            norm1(1)
            row_max(0, 0)
            row_max(0, 1)
            kv_copy(v, v.tensor_copy, 1)
            stats1(2)
            mean_var1(2)
            add_eps1(2)
            normalise(0)
            for t in range(NT):
                before, after, later = t >= 1, t + 1 < NT, t + 2 < NT
                if after:
                    row_max(t + 1, 0)
                    row_max(t + 1, 1)
                if later and t > 0:
                    stats1(t + 2)
                if before:
                    residual(t - 1)
                if later and t > 0:
                    mean_var1(t + 2)
                if before:
                    stats_2(t - 1)
                if later and t > 0:
                    add_eps1(t + 2)
                if before:
                    mean_var2(t - 1)
                if t >= 3:
                    add_gate_bias(t - 3)
                if before:
                    add_eps2(t - 1)
                if t >= 3:
                    top(t - 3)
                if later:
                    norm1(t + 2)
                if t >= 3:
                    top_index(t - 3)
                if before:
                    norm2(t - 1)
                if t >= 3:
                    choose(t - 3)
                if after:
                    normalise(t + 1)
            residual(NT - 1)
            stats_2(NT - 1)
            mean_var2(NT - 1)
            add_eps2(NT - 1)
            route(NT - 3)
            norm2(NT - 1)
            route(NT - 2)
            route(NT - 1)
            v.wait_ge(choice_done, TOPK * NT)

            v.wait_ge(lo_split, PIECES * (E - 1))
            v.wait_ge(count_ps, 1)
            counts = setup_bank[:, 64:64 + E * NT]
            before = setup_bank[:, 0:E * NT].rearrange("p (e t) -> p e t", t=NT)
            chain(v.tensor_tensor_scan(incl[:].rearrange("p e t -> p (e t)"), scan_keep[:], counts, 0.0,
                                       ALU.mult, ALU.add))
            chain(v.tensor_tensor(over[:], incl[:, :, NT - 1:NT].to_broadcast([P, E, NT]),
                                  steps128[:].rearrange("p (a t) -> p a t", a=1).to_broadcast([P, E, NT]), ALU.is_gt))
            chain(v.tensor_reduce(ntile[:], over[:], AX.X, ALU.add))
            chain(v.tensor_tensor_scan(tile_start[:, 1:E + 1], scan_keep[:, 1:2].to_broadcast([P, E]), ntile[:], 0.0,
                                       ALU.mult, ALU.add))
            chain(v.scalar_tensor_tensor(slot0[:], tile_start[:, 0:E].rearrange("p (e a) -> p e a", a=1).to_broadcast([P, E, NT]),
                                         float(P), incl[:], ALU.mult, ALU.add))
            chain(v.tensor_tensor(slot_all[:], before, slot0[:], ALU.add))
            for k in range(TOPK):
                ins = v.tensor_tensor(slot_sel[:, k].rearrange("p t e -> p e t"), chosen[:, k], slot_all[:], ALU.mult)
            chain(ins)
            chain(v.tensor_reduce(slot_f[:], slot_sel[:], AX.X, ALU.add))
            chain(v.tensor_copy(slot_i[:], slot_f[:]))
            v.tensor_scalar(lo_i[:], slot_i[:], P - 1, None, ALU.bitwise_and).then_inc(slots_known, 1)
            chain(v.tensor_scalar(hi_i[:], slot_i[:], 7, None, ALU.arith_shift_right))
            v.tensor_tensor(hi_eq[:], iota_st[:].rearrange("p (a s) -> p a s", a=1).to_broadcast([P, TOPK * NT, ST]),
                            hi_i[:].rearrange("p k (t a) -> p (k t) a", a=1).to_broadcast([P, TOPK * NT, ST]),
                            ALU.is_equal).then_inc(hi_eq_done, 1)
            for t in range(NT):
                v.tensor_scalar(lo_hot[:, 0, t, :], iota_h[:], lo_i[:, 0, t:t + 1], None, ALU.is_equal).then_inc(lo_hot_dve, 1)
                if t < NT - POOL_HOTS:
                    v.tensor_scalar(lo_hot[:, 1, t, :], iota_h[:], lo_i[:, 1, t:t + 1], None, ALU.is_equal).then_inc(lo_hot_dve, 1)
            v.wait_ge(slot_tokens_ps, 1)
            v.tensor_scalar(gather_i[:], small_bank[:, 0:ST], -1.0, 0.0, ALU.add, ALU.max).then_inc(slots_done, 1)
            chain(v.tensor_scalar(empty_f[:], small_bank[:, 0:ST], 0.0, junk_row[:, 0:1], ALU.is_equal, ALU.mult))
            v.wait_ge(slots_done, 1)
            v.tensor_tensor(scatter_i[:], empty_f[:], gather_i[:], ALU.add).then_inc(scatter_ids, 1)

            chain(v.tensor_copy(n_used[:], tile_start[:, E:E + 1]))
            chain(v.tensor_tensor(past[:], iota_st[:].rearrange("p (s a) -> p s a", a=1).to_broadcast([P, ST, E]),
                                  tile_start[:, 1:E + 1].rearrange("p (a e) -> p a e", a=1).to_broadcast([P, ST, E]), ALU.is_ge))
            chain(v.tensor_reduce(exp_f[:], past[:], AX.X, ALU.add))
            v.tensor_scalar(exp_i[:], exp_f[:], float(E - 1), None, ALU.min).then_inc(n_used_done, 1)

            def left_of(j):
                v.wait_ge(hi_turned, j + 1)
                if j >= 2:
                    v.wait_ge(y_ps, j - 1)
                v.tensor_tensor(xgT_lo[:, j % 2, :], turned[:, j % 2, :], xgT_hi[:, j % 2, :].bitcast(F32),
                                ALU.subtract).then_inc(lo_turned, 1)

            def add_bias(j):
                e = v.value_load(exp_i[0:1, j:j + 1], min_val=0, max_val=E - 1)
                v.wait_ge(y_ps, j + 1)
                if j >= NG:
                    v.wait_ge(scattered[j % NG], 16 * (j // NG))
                v.tensor_tensor(ysb[:, j % NG, :], energy[:, j % 2, :],
                                b_rep[:, bass.ds(e, 1), :].rearrange("p b h -> p (b h)"), ALU.add).then_inc(y_biased, 1)

            v.wait_ge(n_used_done, 1)
            used = v.value_load(n_used[0:1, 0:1], min_val=MIN_TILES, max_val=SLOT_TILES)
            v.wait_ge(bias_loaded, 16 * 2)
            left_of(0)
            for j in range(SLOT_TILES):
                if j + 1 < SLOT_TILES:
                    if_used(v, used, j + 1, lambda: left_of(j + 1))
                if_used(v, used, j, lambda: add_bias(j))

        @block.tensor
        def _(pe):
            def keep_busy(n, rows):
                for _ in range(n):
                    pe.matmul(turned[:, 0, :], rows[:, 0:P], rows, start=True, stop=True)

            pe.wait_ge(idle_done, 1)
            keep_busy(START_IDLE, idle_rows[:])
            pe.wait_ge(small_loaded, 16 * 4)
            pe.wait_ge(consts, N_CONST)
            dup = lambda i: w_small[:, i, :, :].rearrange("o r c -> o (r c)")
            pe.matmul(setup_bank[:, 0:C], dup(1), w_small[:, 0, 0, :], start=True, stop=True)
            pe.transpose(setup_bank[:, C:2 * C], dup(2), ident[0:C, 0:C])
            pe.transpose(setup_bank[:, 2 * C:3 * C], dup(3), ident[0:C, 0:C]).then_inc(set_ps, 1)
            keep_busy(SETUP_IDLE, idle_rows[:])

            def keys_values(t):
                if t == 0:
                    pe.wait_ge(ctx_loaded, 16)
                    pe.wait_ge(set_sb, 6)
                else:
                    pe.wait_ge(v_sb, t)
                pe.matmul(kv_bank[:, 0:M], at_diag[:], ctx_sb[:, t, :], start=True, stop=True)
                mm = pe.matmul(kv_bank[:, M:M + P], ctx_sb[:, t, :], wv_diag[:], start=True, stop=True)
                mm.then_inc(kv_ps, 1)

            def energies(t):
                pe.wait_ge(xn_done, t + 1)
                pe.wait_ge(kk_sb, PAIR * (t + 1))
                for h in range(2):
                    if t >= 1:
                        pe.wait_ge(exp_done, 2 * (t - 1) + h + 1)
                    for c in range(2):
                        mm = pe.matmul(energy[:, h, c * PAIR * M:(c + 1) * PAIR * M],
                                       xn[:, t % 2, (2 * h + c) * P:(2 * h + c + 1) * P], kk[:, t % 2, :],
                                       start=True, stop=True)
                    mm.then_inc(energy_ps, 1)

            def skip(t):
                if t >= 1:
                    pe.wait_ge(acc_used, t)
                pe.matmul(acc[:], wskip_diag[:], xn[:, t % 2, :], start=True, stop=False).then_inc(skip_ps, 1)

            def turn_probs(t):
                for j in range(PAIR):
                    pe.wait_ge(probs_done, PAIR * t + j + 1)
                    if t >= 1:
                        pe.wait_ge(turned_sb, PAIR * (t - 1) + j + 1)
                    for c in range(NCH):
                        mm = pe.transpose(turned[:, j, c * P:(c + 1) * P], probs[:, t % 2, c, j, :], ident[:])
                    mm.then_inc(turned_ps, 1)

            def values(t):
                pe.wait_ge(v_sb, t + 1)
                for j in range(PAIR):
                    pe.wait_ge(turned_sb, PAIR * t + j + 1)
                    mm = pe.matmul(acc[:], vext[:, t % 4, j, :], probsT[:, j, :], start=False, stop=(j == PAIR - 1))
                mm.then_inc(acc_ps, 1)

            def gate_turn(t):
                pe.wait_ge(xn2_done, t + 1)
                if t >= 1:
                    pe.wait_ge(xn2T_sb, t)
                for c in range(NCH):
                    mm = pe.transpose(gate_bank[:, c * P:(c + 1) * P], xn2[:, t % 2, c * P:(c + 1) * P], ident[:])
                mm.then_inc(xn2T_ps, 1)

            def gate_logits(t):
                pe.wait_ge(gate_loaded, 32)
                pe.wait_ge(xn2T_sb, t + 1)
                if t >= 1:
                    pe.wait_ge(logits_used, t)
                for c in range(NCH):
                    mm = pe.matmul(small_bank[:, 0:E], xn2T[:, c, :], w_gate[:, c, :], start=(c == 0), stop=(c == NCH - 1))
                mm.then_inc(logits_ps, 1)

            keys_values(0)
            energies(0)
            keys_values(1)
            energies(1)
            keys_values(2)
            for t in range(NT):
                skip(t)
                turn_probs(t)
                if t + 3 < NT:
                    keys_values(t + 3)
                if t + 2 < NT:
                    energies(t + 2)
                values(t)
                if t >= 2:
                    gate_logits(t - 2)
                if t >= 1:
                    gate_turn(t - 1)
            gate_logits(NT - 2)
            gate_turn(NT - 1)
            gate_logits(NT - 1)

            pe.wait_ge(choice_done, TOPK * NT)
            pe.wait_ge(before_done, 1)
            for start, ones in ((0, before_h), (64, ones_h)):
                for k in range(TOPK):
                    mm = pe.matmul(setup_bank[:, start:start + E * NT], ones[:], chosen[:, k].rearrange("p e t -> p (e t)"),
                                   start=(k == 0), stop=(k == TOPK - 1))
            mm.then_inc(count_ps, 1)
            pe.wait_ge(hi_hot_done, 1)
            for t in range(NT):
                for k in range(TOPK):
                    by_pool = max(0, t + 1 - (NT - POOL_HOTS))
                    if k == 1 and by_pool:
                        pe.wait_ge(lo_hot_pool, by_pool)
                    else:
                        pe.wait_ge(lo_hot_dve, TOPK * t + k + 1 - max(0, by_pool - 1))
                    mm = pe.matmul(small_bank[:, 0:ST], lo_hot[:, k, t, :], hi_hot[:, k * NT + t, :],
                                   start=(t == 0 and k == 0), stop=(t == NT - 1 and k == 1))
            mm.then_inc(slot_tokens_ps, 1)
            keep_busy(GATHER_IDLE, lo_hot[:, 0, 0:NCH, :].rearrange("p t i -> p (t i)"))

            def turn(j):
                pe.wait_ge(gathered[j % NG], 16 * (j // NG + 1))
                if j >= 2:
                    pe.wait_ge(lo_turned, j - 1)
                for c in range(NCH):
                    mm = pe.transpose(turned[:, j % 2, c * P:(c + 1) * P], xg[:, j % NG, c * P:(c + 1) * P], ident[:])
                mm.then_inc(xgT_ps, 1)

            pe.wait_ge(n_used_done, 1)
            used = pe.value_load(n_used[0:1, 0:1], min_val=MIN_TILES, max_val=SLOT_TILES)
            pe.wait_ge(hi_split, PIECES * E)
            pe.wait_ge(lo_split, PIECES * E)
            def multiply(j):
                e = pe.value_load(exp_i[0:1, j:j + 1], min_val=0, max_val=E - 1)
                if j >= 2:
                    pe.wait_ge(y_biased, j - 1)
                y = energy[:, j % 2, :]
                for xp, wp, ready in ((xgT_hi, w_hi, hi_turned), (xgT_hi, w_lo, hi_turned), (xgT_lo, w_hi, lo_turned)):
                    pe.wait_ge(ready, j + 1)
                    for c in range(NCH):
                        mm = pe.matmul(y, xp[:, j % 2, c * P:(c + 1) * P],
                                       wp[:, bass.ds(e, 1), c, :].rearrange("p b h -> p (b h)"),
                                       start=(wp is w_hi and xp is xgT_hi and c == 0), stop=(xp is xgT_lo and c == NCH - 1))
                mm.then_inc(y_ps, 1)

            turn(0)
            for j in range(SLOT_TILES):
                if j + 1 < SLOT_TILES:
                    if_used(pe, used, j + 1, lambda: turn(j + 1))
                if_used(pe, used, j, lambda: multiply(j))


_INS = ['x', 'ctx_1024', 'L0_xattn_Wq', 'L0_xattn_Wk', 'L0_xattn_Wv', 'L0_xattn_Wskip', 'L0_ffn_W_gate', 'L0_ffn_b_gate',
        'L0_ffn_W_e', 'L0_ffn_b_e']


def kernel(**inputs):
    import numpy as _np
    import concourse.bacc as _bacc
    from concourse import mybir as _mybir
    from concourse.bass_utils import run_bass_kernel_spmd as _run

    nc = _bacc.Bacc("TRN2", target_bir_lowering=False, num_devices=1)
    arrays, args = {}, []
    for name in _INS:
        a = _np.ascontiguousarray(inputs[name])
        arrays[f"in_{name}_dram"] = a
        args.append(nc.dram_tensor(f"in_{name}_dram", a.shape, _mybir.dt.from_np(a.dtype), kind="ExternalInput").ap())
    B, C, D = inputs["x"].shape
    out = nc.dram_tensor("out_0_dram", (B * C + P, D), _mybir.dt.float32, kind="ExternalOutput").ap()
    build_xattn_moe(nc, *args, out)
    r = _run(nc, [arrays], core_ids=[0])
    return r.results[0]["out_0_dram"][:B * C].reshape(B, C, D)
```
